# Optimizing a Trainium2 kernel written in Bass

```python
import numpy as np
import jax
import jax.numpy as jnp

def _softmax(x, axis=-1):
    return jax.nn.softmax(x, axis=axis)

def _gelu(x):
    return jax.nn.gelu(x, approximate=True)

def _silu(x):
    return jax.nn.silu(x)

def _sigmoid(x):
    return jax.nn.sigmoid(x)

def _layernorm(x, axis=-1, eps=1e-05):
    m = jnp.mean(x, axis=axis, keepdims=True)
    v = jnp.var(x, axis=axis, keepdims=True)
    return (x - m) / jnp.sqrt(v + eps)

def _scatter_add(tgt, idx, src, axis=0):
    return tgt.at[idx].add(src)

def _segment_sum(src, seg, n):
    return jax.ops.segment_sum(src, seg, n)
kernel_name = 'mk_flamingo_gated_d1_seqx_r4_8d9d30'

def setup_inputs(seed: int=0):
    np.random.seed(seed)
    _w = jnp.asarray

    def _rec_inputs():
        import jax
        import jax.numpy as jnp
        _rk = jax.random.key(seed)
        x = -0.0005207 + 1.001 * jax.random.normal(jax.random.fold_in(_rk, 1), (2, 1024, 256), jnp.float32)
        _lenS = 1024 - jax.random.randint(jax.random.fold_in(_rk, 7), (2,), 0, max(1, 1024 // 4) + 1, jnp.int32)
        _lenS2 = 77 - jax.random.randint(jax.random.fold_in(_rk, 8), (2,), 0, max(1, 77 // 4) + 1, jnp.int32)
        _ctx_1024P = jax.random.normal(jax.random.fold_in(_rk, 12), (2, 16, 256), jnp.float32)
        _ctx_1024c = jax.random.dirichlet(jax.random.fold_in(_rk, 512), 0.3 * jnp.ones((16,), jnp.float32), (2, 77))
        _ctx_1024t = jnp.einsum('bsk,bkd->bsd', _ctx_1024c, _ctx_1024P)
        _ctx_1024t = _ctx_1024t * jax.lax.rsqrt(jnp.mean(jnp.square(_ctx_1024t)) + 1e-12) * 0.953939
        ctx_1024 = 0.00191187 + 0.999416 * (_ctx_1024t + 0.3 * jax.random.normal(jax.random.fold_in(_rk, 612), (2, 77, 256), jnp.float32))
        _validS = jnp.arange(1024)[None, :] < _lenS[:, None]
        _validS2 = jnp.arange(77)[None, :] < _lenS2[:, None]
        _causal = jnp.tril(jnp.ones((1024, 1024), dtype=bool))
        mask_BxS_ff1 = jnp.where(jnp.ones((2, 1024), dtype=bool), 1.0, 0.0).astype(jnp.float32)
        mask_BxS2_ik0 = jnp.where(jnp.broadcast_to(_validS2[:, :], (2, 77)), 0, 1).astype(jnp.int32)
        _g = jax.random.normal(jax.random.fold_in(_rk, 9001), (2, 1), jnp.float32)
        _g = jnp.sign(_g) * jnp.maximum(jnp.abs(_g), 1.0) + (_g == 0) * 1.0
        g_xattn = _g[0]
        g_ffn = _g[1]
        return (x, ctx_1024, mask_BxS_ff1, mask_BxS2_ik0, g_xattn, g_ffn)
    x, ctx_1024, mask_BxS_ff1, mask_BxS2_ik0, g_xattn, g_ffn = _rec_inputs()

    def _L0_xattn_setup():
        import jax, jax.numpy as jnp
        import numpy as np
        B, F, T, D = (8, 64, 32, 256)
        NEG = -1e+30
        key = jax.random.key(seed)
        ks = jax.random.split(key, 10)
        s = 1.0 / np.sqrt(D)
        return {'features': jax.random.normal(ks[0], (B, F, D), jnp.float32), 'masks': jnp.ones((B, F), jnp.float32), 'textual_features': jax.random.normal(ks[1], (B, T, D), jnp.float32), 'q_masks': jax.random.randint(ks[2], (B, T), 0, 2, jnp.int32), 'Ws': jax.random.normal(ks[3], (D, D), jnp.float32) * s, 'W': jax.random.normal(ks[4], (D, D), jnp.float32) * s, 'w': jax.random.normal(ks[5], (D, 1), jnp.float32) * s, 'b': jax.random.normal(ks[6], (1, D), jnp.float32) * s, 'Wcw': jax.random.normal(ks[7], (1, D), jnp.float32) * s, 'bcw': jnp.zeros((1,), jnp.float32), 'Wcb': jax.random.normal(ks[8], (1, D), jnp.float32) * s, 'bcb': jnp.zeros((1,), jnp.float32)}
    _L0_xattn_all = _L0_xattn_setup()
    _L0_xattn_in = {k: v for k, v in _L0_xattn_all.items() if k in ('Ws', 'W', 'w', 'b', 'Wcw', 'bcw', 'Wcb', 'bcb')}
    del _L0_xattn_all

    def _L0_ffn_setup():
        import jax, jax.numpy as jnp
        import numpy as np
        B, S, D, E, K = (4, 512, 256, 8, 2)
        H = 4 * D
        key = jax.random.key(seed)
        k0, k1, k2, k3 = jax.random.split(key, 4)
        x = jax.random.normal(k0, (B, S, D), dtype=jnp.float32)
        router_w = jax.random.normal(k1, (E, D), dtype=jnp.float32) * 0.02
        w1 = jax.random.normal(k2, (E, H, D), dtype=jnp.float32) * 0.02
        w2 = jax.random.normal(k3, (E, D, H), dtype=jnp.float32) * 0.02
        return {'x': x, 'router_w': router_w, 'w1': w1, 'w2': w2}
    _L0_ffn_all = _L0_ffn_setup()
    _L0_ffn_in = {k: v for k, v in _L0_ffn_all.items() if k in ('router_w', 'w1', 'w2')}
    del _L0_ffn_all
    return {'x': x, 'ctx_1024': ctx_1024, 'mask_BxS_ff1': mask_BxS_ff1, 'mask_BxS2_ik0': mask_BxS2_ik0, 'g_xattn': g_xattn, 'g_ffn': g_ffn, 'L0_xattn_Ws': _L0_xattn_in['Ws'], 'L0_xattn_W': _L0_xattn_in['W'], 'L0_xattn_w': _L0_xattn_in['w'], 'L0_xattn_b': _L0_xattn_in['b'], 'L0_xattn_Wcw': _L0_xattn_in['Wcw'], 'L0_xattn_bcw': _L0_xattn_in['bcw'], 'L0_xattn_Wcb': _L0_xattn_in['Wcb'], 'L0_xattn_bcb': _L0_xattn_in['bcb'], 'L0_ffn_router_w': _L0_ffn_in['router_w'], 'L0_ffn_w1': _L0_ffn_in['w1'], 'L0_ffn_w2': _L0_ffn_in['w2']}

def reference(x, ctx_1024, mask_BxS_ff1, mask_BxS2_ik0, g_xattn, g_ffn, L0_xattn_Ws, L0_xattn_W, L0_xattn_w, L0_xattn_b, L0_xattn_Wcw, L0_xattn_bcw, L0_xattn_Wcb, L0_xattn_bcb, L0_ffn_router_w, L0_ffn_w1, L0_ffn_w2):
    import jax
    import jax.numpy as jnp

    def _L0_xattn_ref(features, masks, textual_features, q_masks, Ws, W, w, b, Wcw, bcw, Wcb, bcb):
        import jax, jax.numpy as jnp
        import numpy as np
        B, F, T, D = (8, 64, 32, 256)
        NEG = -1e+30
        txt_proj = jnp.einsum('btd,de->bte', textual_features, Ws)
        feat_proj = jnp.einsum('bfd,de->bfe', features, W)
        h = jnp.tanh(txt_proj[:, None, :, :] + feat_proj[:, :, None, :] + b[None, None, :, :][..., 0, :])
        rho = jnp.einsum('bftd,d->bft', h, w[:, 0])
        qm = q_masks.astype(jnp.float32)
        rho = rho + (1.0 - qm)[:, None, :] * NEG
        att = jax.nn.softmax(rho, axis=-1)
        txt_h = jnp.einsum('bft,btd->bfd', att, textual_features)
        w_s = jnp.tanh(jnp.einsum('bfd,od->bfo', txt_h, Wcw) + bcw)
        b_s = jnp.tanh(jnp.einsum('bfd,od->bfo', txt_h, Wcb) + bcb)
        return w_s * features + b_s

    def _L0_ffn_ref(x, router_w, w1, w2):
        import jax, jax.numpy as jnp
        import numpy as np
        B, S, D, E, K = (4, 512, 256, 8, 2)
        H = 4 * D
        b, s, d = x.shape
        e = router_w.shape[0]
        logits = jnp.einsum('bsd,ed->bse', x, router_w)
        probs = jax.nn.softmax(logits, axis=-1)
        topk_vals, topk_idx = jax.lax.top_k(probs, K)
        x_flat = x.reshape(b * s, d)
        vals = topk_vals.reshape(b * s, K)
        idx = topk_idx.reshape(b * s, K)
        out = jnp.zeros_like(x_flat)
        for eid in range(e):
            w = jnp.sum(jnp.where(idx == eid, vals, jnp.zeros((), x.dtype)), axis=-1)
            h = jax.nn.gelu(x_flat @ w1[eid].T, approximate=False)
            y = h @ w2[eid].T
            out = out + w[:, None] * y
        return out.reshape(b, s, d)
    x = x + jnp.tanh(g_xattn[0]) * _L0_xattn_ref(_layernorm(x, axis=-1), mask_BxS_ff1, ctx_1024, mask_BxS2_ik0, L0_xattn_Ws, L0_xattn_W, L0_xattn_w, L0_xattn_b, L0_xattn_Wcw, L0_xattn_bcw, L0_xattn_Wcb, L0_xattn_bcb)
    x = x + jnp.tanh(g_ffn[0]) * _L0_ffn_ref(_layernorm(x, axis=-1), L0_ffn_router_w, L0_ffn_w1, L0_ffn_w2)
    return x

_drawn_inputs = setup_inputs


def setup_inputs(seed=0):
    import zlib

    import numpy as np

    out = dict(_drawn_inputs(seed))
    spreads = {}
    factors = {'L0_xattn_b': 8.0, 'L0_ffn_router_w': 2.678}
    for name, (base, spread) in spreads.items():
        noise = np.random.default_rng([zlib.crc32(name.encode()), seed]).standard_normal(out[name].shape)
        drawn = base * np.exp(spread * noise) if base else spread * noise
        out[name] = jnp.asarray(drawn.astype(out[name].dtype))
    for name, factor in factors.items():
        out[name] = (out[name] * factor).astype(out[name].dtype)
    return out
```

```python
from contextlib import ExitStack

import concourse.bass as bass
from concourse import mybir

ALU = mybir.AluOpType
ACT = mybir.ActivationFunctionType
AX = mybir.AxisListType
F32 = mybir.dt.float32
I32 = mybir.dt.int32
U32 = mybir.dt.uint32

P = 128
B, S, D, T = 2, 1024, 256, 77
E, H = 8, 1024
DC, HC = D // P, H // P
NTOK = B * S
QT = 512
NQ, TPQ = NTOK // QT, QT // P
CG = 4
RS = -(-T // CG)
TP = RS * CG
NBLK = RS * DC
HB = 4
NEG = 1e30
FILL = -3e38
EPS = 1e-5

GROUPS = ((0, 1), (1, NQ))
CAP = [(b - a) * QT + P for a, b in GROUPS]
ROW0 = [0, E * CAP[0] + (E - 1) * P]
NROWS = ROW0[1] + E * CAP[1] + (E - 1) * P
NTILES = [2 * (b - a) * QT // P + E - 1 for a, b in GROUPS]
NT_A, NT = NTILES[0], sum(NTILES)
META = 1 + E
ROW = D + META

FQ = 4
STEP = 9
TA = 1 + 2 * FQ
TB = 1 + NT_A
TE = 1 + NT
S_LINKS = 27
P_LINKS = 1
R_LINKS = 9


def in_register(eng, value):
    return value if isinstance(value, int) else eng.to_reg(value)


class Link:

    def __init__(self, eng, sem, base):
        self.eng, self.sem, self.base, self.n = eng, sem, base, 0

    def __call__(self, ins, first=None):
        self.n += 1
        ins.then_inc(self.sem, 1)
        value = self.base + self.n
        if first:
            value = in_register(self.eng, value)
            self.eng.wait_ge(*first)
        self.eng.wait_ge(self.sem, value)


def flamingo_moe(nc, x, ctxT, mask, g_xattn, g_ffn, Ws, W, w, b, Wcw, bcw, Wcb, bcb, router, w1, w2, out):
    with ExitStack() as ctx:
        def sb(name, shape, dt=F32):
            return ctx.enter_context(nc.sbuf_tensor(name, shape, dt))

        def sem(name):
            return ctx.enter_context(nc.semaphore(name))

        w1_sb = sb("w1_sb", [P, E, DC, H])
        w2_sb = sb("w2_sb", [P, E, HC, D])
        featT = sb("featT", [P, DC, NQ, QT])
        hbuf = sb("hbuf", [P, HB, CG, QT])
        x_res = sb("x_res", [P, TPQ, D])
        x2T = sb("x2T", [P, DC, QT])
        rows = sb("rows", [P, TPQ, ROW])
        W_sb = sb("W_sb", [P, DC, D])
        sc = sb("sc", [P, TPQ, TP])
        tmp = sb("tmp", [P, 2, TPQ, TP])
        rhoT = tmp[:].rearrange("p a t c -> p (a t c)")[:, 0:QT]
        ident = sb("ident", [P, P])
        before = sb("before", [P, P])
        ones = sb("ones", [P, P])
        wpad = sb("wpad", [P, DC, 64])
        txtb = sb("txtb", [P, DC, B, TP])
        cwb = sb("cwb", [P, B, 2, TP])
        mneg = sb("mneg", [P, B, TP])
        cols = sb("cols", [P, 4, DC])
        rT = sb("rT", [P, DC, E])
        gs = sb("gs", [P, 4])
        tg = sb("tg", [P, 2])
        negh = sb("negh", [P, TPQ])
        stats = sb("stats", [P, TPQ, 6])
        mv = sb("mv", [P, NTOK // P, 2])
        var = sb("var", [P, TPQ])
        rstd = sb("rstd", [P, NTOK // P])
        stats2 = sb("stats2", [P, TPQ, 6])
        mv2 = sb("mv2", [P, TPQ, 2])
        var2 = sb("var2", [P, TPQ])
        rstd2 = sb("rstd2", [P, TPQ])
        mx = sb("mx", [P, TPQ])
        den = sb("den", [P, TPQ])
        ws = sb("ws", [P, 2, TPQ])
        wt = sb("wt", [P, 2, TPQ])
        ab = sb("ab", [P, 3, TPQ])
        lg = sb("lg", [P, TPQ, E])
        top = sb("top", [P, TPQ, E])
        topi = sb("topi", [P, TPQ, E], U32)
        topf = sb("topf", [P, TPQ, 2])
        pick = sb("pick", [P, 3, TPQ, E])
        dl = sb("dl", [P, TPQ, E])
        zs = sb("zs", [P, TPQ])
        cum = sb("cum", [P, TPQ + 1, E])
        pos = sb("pos", [P, TPQ, E])
        sel = tmp[:].rearrange("p a t c -> p (a t c)")[:, 0:2 * TPQ * E].rearrange(
            "p (a t e) -> p a t e", a=2, t=TPQ)
        slotf = sb("slotf", [P, 2, TPQ])
        slot = sb("slot", [P, 2, TPQ], I32)
        region = sb("region", [P, 2, E])
        tokid = sb("tokid", [P, NTOK // P], I32)
        iota8 = sb("iota8", [P, E])
        iotan = sb("iotan", [P, NTILES[1]])
        tl_i = sb("tl_i", [P, E], I32)
        tl = sb("tl", [P, 2, E])
        ind = tmp[:].rearrange("p a t c -> p (a t c)")[:, 0:2 * NTILES[1] * E].rearrange(
            "p (a n e) -> p a n e", a=2, n=NTILES[1])
        tabf = sb("tabf", [P, 3, NTILES[1]])
        tab_e = sb("tab_e", [P, 1 + NT], I32)
        tab_r = sb("tab_r", [P, 1 + NT], I32)
        pad_r = sb("pad_r", [P, 2, E], I32)
        pad = sb("pad", [P, ROW])
        xs = sb("xs", [P, 2, ROW])
        xsT = sb("xsT", [P, DC, P])
        meta = sb("meta", [P, 2, META])
        hg = sb("hg", [P, H])
        hgT = sb("hgT", [P, HC, P])
        y_sb = sb("y_sb", [P, D])
        xp = hg[:].rearrange("p (t d) -> p t d", t=TPQ)
        xnT = hgT[:].rearrange("p c d -> p (c d)").rearrange("p (c k) -> p c k", c=DC)
        Ws_sb = x2T[:].rearrange("p c k -> p (c k)")[:, 0:DC * D].rearrange("p (c d) -> p c d", c=DC)
        ctx_sb = x2T[:].rearrange("p c k -> p (c k)")[:, DC * D:DC * (D + B * TP)].rearrange("p (c t) -> p c t", c=DC)
        wrep = x_res[:].rearrange("p t d -> p (t d)")[:, 0:2 * DC * P].rearrange("p (k c m) -> p k c m", k=2, c=DC)
        mask_i = sc[:, 0:B, :].bitcast(I32)
        xn = rows[:, :, 0:D]
        scratch = nc.dram_tensor("row_scratch", [NROWS, ROW], F32, kind="Internal").ap()

        def bank(name, n=1):
            return ctx.enter_context(nc.psum_tensor(name, [P, n * 512], F32))

        rho = bank("rho")
        misc = [bank("misc0"), bank("misc1")]
        h_ps = bank("h_ps", 2)
        hT_ps = bank("hT_ps", 2)
        y_bank = bank("y_bank")
        y_ps = y_bank[:, 0:D]
        xsT_ps = hT_ps[:, 0:D]

        consts_in = sem("consts_in")
        x_in = sem("x_in")
        w_in = sem("w_in")
        fill_in = sem("fill_in")
        pads_in = sem("pads_in")
        pool_const = sem("pool_const")
        dve_const = sem("dve_const")
        gate_t = sem("gate_t")
        setup_ps = sem("setup_ps")
        setup_sb = sem("setup_sb")
        p_link = sem("p_link")
        mv_ok = sem("mv_ok")
        s_link = sem("s_link")
        r_link = sem("r_link")
        var1_ok = sem("var1_ok")
        rstd1_ok = sem("rstd1_ok")
        xn_ok = sem("xn_ok")
        xnT_ps_ok = sem("xnT_ps_ok")
        xnT_sb_ok = sem("xnT_sb_ok")
        feat_ps_ok = sem("feat_ps_ok")
        feat_sb_ok = sem("feat_sb_ok")
        sum_ok = sem("sum_ok")
        h_ok = sem("h_ok")
        h_used = sem("h_used")
        rhoT_ok = sem("rhoT_ok")
        rho_ps_ok = sem("rho_ps_ok")
        shifted_ok = sem("shifted_ok")
        exp_ok = sem("exp_ok")
        ws_ok = sem("ws_ok")
        wt_ok = sem("wt_ok")
        xres_in = sem("xres_in")
        x1_ok = sem("x1_ok")
        x1_out = sem("x1_out")
        rstd2_ok = sem("rstd2_ok")
        x2_ok = sem("x2_ok")
        x2T_ps_ok = sem("x2T_ps_ok")
        x2T_sb_ok = sem("x2T_sb_ok")
        lg_ps_ok = sem("lg_ps_ok")
        pick_ok = sem("pick_ok")
        rexp_ok = sem("rexp_ok")
        count_ps_ok = sem("count_ps_ok")
        rows_ok = sem("rows_ok")
        scattered = sem("scattered")
        table_ok = sem("table_ok")
        xs_in = [sem("xs_in0"), sem("xs_in1")]
        xsT_ps_ok = sem("xsT_ps_ok")
        xsT_ok = sem("xsT_ok")
        h_ps_ok = sem("h_ps_ok")
        hg_ok = sem("hg_ok")
        hT_ps_ok = sem("hT_ps_ok")
        hT_ok = sem("hT_ok")
        meta_ok = sem("meta_ok")
        y_ps_ok = sem("y_ps_ok")
        y_ok = sem("y_ok")
        added = sem("added")

        N_CONST = 1 + 1 + 1 + 4 + 4 + 1 + B
        POOL_CONSTS = 11
        DVE_CONSTS = 5
        x_rows = x.rearrange("b s d -> (b s) d").rearrange("(t p) d -> p t d", p=P)
        out_rows = out.rearrange("(t p) d -> p t d", p=P)

        PE_P = {12 * k + d: (k + 1, s) for k in range(NQ - 1) for d, s in ((1, "turn"), (5, "project"))}
        DVE_P = {12 * k + d: (k + 1, s) for k in range(NQ - 1)
                 for d, s in ((1, "stats"), (3, "norm"), (7, "turned"), (11, "projected"))}
        PE_S = {0: "turn_scores", 18: "turn_x2", 21: "logits", 25: "count"}
        ACT_S = {7: "exp", 12: "tanh", 25: "exp_router"}
        DVE_S = {3: "scores_out", 6: "mask", 12: "gates", 17: "x1", 20: "x2", 23: "x2T", 26: "top2", 30: "place"}
        DIRECT = range(0, NBLK, 1)
        PE_F = {STEP * m + d: (m, s) for m in range(FQ)
                for d, s in ((0, "up0"), (1, "up1"), (3, "turn_x"), (4, "down"), (6, "turn_h"))}
        ACT_F = {STEP * m + d: (m, s) for m in range(FQ) for d, s in ((2, "gelu0"), (3, "gelu1"))}
        DVE_F = {STEP * m + d: (m, s) for m in range(FQ) for d, s in ((6, "x"), (9, "h"), (10, "y"))}

        def summed(k):
            n = CG if k // DC < RS - 1 else T - CG * (RS - 1)
            return n, n - (1 if n == CG and k in DIRECT else 0)

        def tile(q, m):
            return FQ * (q - 2) + 1 + m, (1 + m) % 2, FQ // 2 * (q - 2) + (m + 2) // 2

        def tile_at(i):
            return i, i % 2, (i + 1) // 2

        def tile_pair(n, u):
            return TB + 2 * n + u, (TB + u) % 2, n + (TB + u + 1) // 2

        PAIRS = (TE - 1 - TB) // 2
        assert (TE - 1 - TB) % 2 == 0 and FQ % 2 == 0

        block = ctx.enter_context(nc.Block())

        @block.sync
        def _(sp):
            sp.dma_start(xp, x_rows[:, 0:TPQ, :]).then_inc(x_in, 16)
            sp.dma_start(W_sb[:], W.rearrange("(c p) e -> p c e", p=P)).then_inc(consts_in, 16)
            sp.dma_start(Ws_sb, Ws.rearrange("(c p) e -> p c e", p=P)).then_inc(consts_in, 16)
            sp.dma_start(ctx_sb.rearrange("p c (b t) -> p (c b) t", b=B)[:, :, 0:T], ctxT).then_inc(consts_in, 16)
            for n, v in enumerate((w, b, Wcw, Wcb)):
                sp.dma_start(cols[:, n, :], v).then_inc(consts_in, 16)
            for n, v in enumerate((g_xattn, g_ffn, bcw, bcb)):
                sp.dma_start(gs[:, n:n + 1], v.partition_broadcast(P)).then_inc(consts_in, 16)
            sp.dma_start(rT[:], router).then_inc(consts_in, 16)
            for bb in range(B):
                sp.dma_start(mask_i[:, bb, 0:T], mask[bb].partition_broadcast(P)).then_inc(consts_in, 16)
            for q in range(1, NQ):
                sp.wait_ge(xn_ok, q)
                sp.dma_start(xp, x_rows[:, TPQ * q:TPQ * (q + 1), :]).then_inc(x_in, 16)
            for e in range(E):
                sp.dma_start(w1_sb[:, e], w1[:, e]).then_inc(w_in, 16)
                sp.dma_start(w2_sb[:, e], w2[:, e]).then_inc(w_in, 16)
            sp.wait_ge(pool_const, POOL_CONSTS)
            for g in range(2):
                for n in range(E - 1):
                    r0 = ROW0[g] + E * CAP[g] + n * P
                    sp.dma_start(scratch[r0:r0 + P, :], pad[:]).then_inc(fill_in, 16)

            def res_load(q, first=False):
                if first:
                    sp.wait_ge(setup_ps, 4)
                else:
                    sp.wait_ge(x1_out, 16 * q)
                    sp.wait_ge(x2_ok, q)
                sp.dma_start(x_res[:], x_rows[:, bass.ds(TPQ * q, TPQ), :]).then_inc(xres_in, 16)

            def x1_store(q):
                sp.wait_ge(x1_ok, q + 1)
                sp.dma_start(out_rows[:, bass.ds(TPQ * q, TPQ), :], x_res[:]).then_inc(x1_out, 16)

            def group_pads(g):
                sp.wait_ge(table_ok, g + 1)
                for e in range(E):
                    r = sp.value_load(pad_r[0:1, g, e:e + 1], min_val=0, max_val=NROWS - P)
                    sp.dma_start(scratch[bass.ds(r, P), :], pad[:]).then_inc(pads_in, 16)
                sp.wait_ge(pads_in, 16 * E * (g + 1))
                sp.wait_ge(scattered, 16 * 2 * TPQ * GROUPS[g][1])

            def xs_load(i, par, half, first=False):
                if not first:
                    sp.wait_ge(meta_ok, i - 1)
                r = sp.value_load(tab_r[0:1, bass.ds(i, 1)], min_val=0, max_val=NROWS - P)
                sp.dma_start(xs[:, par, :], scratch[bass.ds(r, P), :]).then_inc(xs_in[par], 16)

            res_load(0, first=True)
            x1_store(0)
            sp.wait_ge(fill_in, 16 * 2 * (E - 1))
            group_pads(0)
            xs_load(*tile_at(1), first=True)
            xs_load(*tile_at(2), first=True)
            with sp.Fori(2, NQ) as q:
                res_load(q - 1)
                for m in range(FQ):
                    if m == 1:
                        x1_store(q - 1)
                    xs_load(*tile(q, m + 2))
            res_load(NQ - 1)
            for i in range(TA, TB - 2):
                if i == TA + 1:
                    x1_store(NQ - 1)
                xs_load(*tile_at(i + 2))
            group_pads(1)
            xs_load(*tile_at(TB))
            xs_load(*tile_at(TB + 1))
            with sp.Fori(0, PAIRS - 1) as n:
                xs_load(*tile_pair(n + 1, 0))
                xs_load(*tile_pair(n + 1, 1))
            xs_load(*tile_at(TE - 1))
            sp.wait_ge(x1_out, 16 * NQ)

        @block.gpsimd
        def _(pool):
            g = nc.gpsimd
            g.memset(negh[:], -0.5).then_inc(pool_const, 1)
            g.memset(ident[:], 0.0).then_inc(pool_const, 1)
            g.memset(ones[:], 1.0).then_inc(pool_const, 1)
            pool.wait_ge(pool_const, 3)
            g.affine_select(out=ident[:], in_=ident[:], compare_op=ALU.not_equal, fill=1.0, base=0,
                            pattern=[[-1, P]], channel_multiplier=1).then_inc(pool_const, 1)
            g.affine_select(out=before[:], in_=ones[:], compare_op=ALU.is_gt, fill=0.0, base=0,
                            pattern=[[1, P]], channel_multiplier=-1).then_inc(pool_const, 1)
            g.iota(tokid[:], pattern=[[P, NTOK // P]], base=0, channel_multiplier=1).then_inc(pool_const, 1)
            g.iota(iota8[:], pattern=[[1, E]], base=0, channel_multiplier=0,
                   allow_small_or_imprecise_dtypes=True).then_inc(pool_const, 1)
            g.iota(iotan[:], pattern=[[1, NTILES[1]]], base=0, channel_multiplier=0,
                   allow_small_or_imprecise_dtypes=True).then_inc(pool_const, 1)
            g.memset(pad[:], 0.0).then_inc(pool_const, 1)
            g.memset(tab_e[:, 0:1], 0).then_inc(pool_const, 1)
            pool.wait_ge(pool_const, 9)
            g.iota(pad[:, D:D + 1].bitcast(I32), pattern=[[0, 1]], base=NTOK,
                   channel_multiplier=1).then_inc(pool_const, 1)

            pool.wait_ge(pool_const, POOL_CONSTS)
            pool.dma_start(out[NTOK:NTOK + P, :], pad[:, 0:D]).then_inc(added, 16)

            for q in range(NQ):
                pool.wait_ge(var1_ok, q + 1)
                g.tensor_tensor(rstd[:, TPQ * q:TPQ * (q + 1)], var[:], negh[:], ALU.pow).then_inc(rstd1_ok, 1)

            def root(q):
                pool.wait_ge(x1_ok, q + 1)
                g.tensor_tensor(rstd2[:], var2[:], negh[:], ALU.pow).then_inc(rstd2_ok, 1)

            def scatter(q):
                count = in_register(pool, q + 1)
                pool.wait_ge(pool_const, POOL_CONSTS)
                pool.wait_ge(rows_ok, count)
                for t in range(TPQ):
                    for k in range(2):
                        g.indirect_dma_start(
                            out=scratch, out_offset=bass.IndirectOffsetOnAxis(ap=slot[:, k, t:t + 1], axis=0),
                            in_=rows[:, t, :], in_offset=None).then_inc(scattered, 16)

            def add(i, par, half, stored=1):
                y_count, add_count = in_register(pool, i + 2), in_register(pool, 16 * (i + 1))
                pool.wait_ge(x1_out, 16 * stored)
                pool.wait_ge(y_ok, y_count)
                pool.wait_ge(added, add_count)
                g.indirect_dma_start(
                    out=out, out_offset=bass.IndirectOffsetOnAxis(ap=meta[:, par, 0:1].bitcast(I32), axis=0),
                    in_=y_sb[:], in_offset=None, compute_op=ALU.add).then_inc(added, 16)

            root(0)
            scatter(0)
            with pool.Fori(2, NQ) as q:
                add(*tile(q, -1))
                root(q - 1)
                add(*tile(q, 0))
                add(*tile(q, 1))
                scatter(q - 1)
                add(*tile(q, 2))
            for i in range(TA, TB):
                if i == TA + 1:
                    root(NQ - 1)
                add(*tile_at(i - 1))
                if i == TA + 4:
                    scatter(NQ - 1)
            with pool.Fori(0, PAIRS) as n:
                add(*tile_pair(n, -1), stored=NQ)
                add(*tile_pair(n, 0), stored=NQ)
            add(*tile_at(TE - 2), stored=NQ)
            add(*tile_at(TE - 1), stored=NQ)
            pool.wait_ge(added, 16 * (TE + 1))

        @block.scalar
        def _(act):
            s = nc.scalar
            act.wait_ge(consts_in, 16 * N_CONST)
            s.activation(tg[:], gs[:, 0:2], ACT.Tanh).then_inc(gate_t, 1)

            def tanh_block(q, k, bb):
                act.wait_ge(sum_ok, NBLK * q + k + 1)
                n, m = summed(k)
                r, c = k // DC, k % DC
                h = hbuf[:, k % HB, 0:m, :]
                ins = s.activation(h, h, ACT.Tanh)
                for j in range(m, n):
                    ins = s.activation(hbuf[:, k % HB, j, :], featT[:, c, bass.ds(q, 1), :].rearrange("p o t -> p (o t)"),
                                       ACT.Tanh, bias=txtb[:, c, bb, CG * r + j:CG * r + j + 1])
                ins.then_inc(h_ok, 1)

            def settle(step, q):
                if step == "exp":
                    act.wait_ge(shifted_ok, q + 1)
                    s.activation(sc[:], sc[:], ACT.Exp).then_inc(exp_ok, 1)
                elif step == "tanh":
                    act.wait_ge(ws_ok, q + 1)
                    s.activation(wt[:], ws[:], ACT.Tanh).then_inc(wt_ok, 1)
                elif step == "exp_router":
                    act.wait_ge(pick_ok, q + 1)
                    s.activation(dl[:], dl[:], ACT.Exp).then_inc(rexp_ok, 1)

            def gelu(i, c):
                act.wait_ge(h_ps_ok, 2 * (i - 1) + c + 1)
                s.activation(hg[:, 512 * c:512 * (c + 1)], h_ps[:, 512 * c:512 * (c + 1)],
                             ACT.Gelu).then_inc(hg_ok, 1)

            def quarter(q, bb, settling, tiles):
                for k in range(NBLK):
                    tanh_block(q, k, bb)
                    if settling and k in ACT_S:
                        settle(ACT_S[k], q - 1)
                    if tiles and k in ACT_F:
                        m, step = ACT_F[k]
                        gelu(tile(q, m)[0], int(step[-1]))

            quarter(0, 0, False, False)
            quarter(1, 0, True, False)
            with act.Fori(2, NQ) as q:
                quarter(q, 1, True, True)
            for i in range(TA, TB):
                if i == TA:
                    settle("exp", NQ - 1)
                    settle("tanh", NQ - 1)
                gelu(i, 0)
                gelu(i, 1)
                if i == TA + 3:
                    settle("exp_router", NQ - 1)
            with act.Fori(0, PAIRS) as n:
                for u in range(2):
                    gelu(tile_pair(n, u)[0], 0)
                    gelu(tile_pair(n, u)[0], 1)
            gelu(TE - 1, 0)
            gelu(TE - 1, 1)

        @block.tensor
        def _(pe):
            t = nc.tensor

            pe.wait_ge(consts_in, 16 * N_CONST)
            pe.wait_ge(dve_const, 2)
            for e in range(DC):
                for c in range(DC):
                    ins = t.matmul(misc[0][:, e * B * TP:(e + 1) * B * TP], Ws_sb[:, c, e * P:(e + 1) * P],
                                   ctx_sb[:, c, :], start=(c == 0), stop=(c == DC - 1))
                ins.then_inc(setup_ps, 1)
            pe.wait_ge(dve_const, DVE_CONSTS)
            for k in range(2):
                for c in range(DC):
                    ins = t.matmul(misc[1][:, k * B * TP:(k + 1) * B * TP], wrep[:, k, c, :],
                                   ctx_sb[:, c, :], start=(c == 0), stop=(c == DC - 1))
                ins.then_inc(setup_ps, 1)

            def prepare(step, q):
                if step == "turn":
                    pe.wait_ge(xn_ok, q + 1)
                    for c in range(DC):
                        if q:
                            pe.wait_ge(feat_sb_ok, DC * (q - 1) + c + 1)
                        for n in range(TPQ):
                            ins = t.transpose(misc[c][:, n * P:(n + 1) * P], xn[:, n, c * P:(c + 1) * P], ident[:])
                        ins.then_inc(xnT_ps_ok, 1)
                elif step == "project":
                    for e in range(DC):
                        pe.wait_ge(xnT_sb_ok, DC * (q + 1))
                        for c in range(DC):
                            ins = t.matmul(misc[e][:], W_sb[:, c, e * P:(e + 1) * P], xnT[:, c, :],
                                           start=(c == 0), stop=(c == DC - 1))
                        ins.then_inc(feat_ps_ok, 1)

            def rho_block(q, k):
                r, c = k // DC, k % DC
                pe.wait_ge(h_ok, NBLK * q + k + 1)
                n = CG if r < RS - 1 else T - CG * (RS - 1)
                for j in range(n):
                    last = r == RS - 1 or (r == RS - 2 and j >= T - CG * (RS - 1))
                    ins = t.matmul(rho[32 * j:32 * j + 32, :], wpad[:, c, 31 - r:63 - r], hbuf[:, k % HB, j, :],
                                   start=(k == 0), stop=(last and c == DC - 1), skip_group_check=True)
                ins.then_inc(h_used, 1)

            def settle(step, q):
                if step == "turn_scores":
                    pe.wait_ge(rhoT_ok, q + 1)
                    for n in range(TPQ):
                        ins = t.transpose(misc[0][:, n * P:(n + 1) * P], rhoT[:, n * P:(n + 1) * P], ident[:])
                    ins.then_inc(rho_ps_ok, 1)
                elif step == "turn_x2":
                    pe.wait_ge(x2_ok, q + 1)
                    for c in range(DC):
                        for n in range(TPQ):
                            ins = t.transpose(misc[c][:, n * P:(n + 1) * P], rows[:, n, c * P:(c + 1) * P], ident[:])
                        ins.then_inc(x2T_ps_ok, 1)
                elif step == "logits":
                    pe.wait_ge(x2T_sb_ok, DC * (q + 1))
                    for n in range(TPQ):
                        for c in range(DC):
                            ins = t.matmul(misc[0][:, n * E:(n + 1) * E], x2T[:, c, n * P:(n + 1) * P],
                                           rT[:, c, :], start=(c == 0), stop=(c == DC - 1))
                    ins.then_inc(lg_ps_ok, 1)
                elif step == "count":
                    pe.wait_ge(pick_ok, q + 1)
                    m = pick[:, 2].rearrange("p t e -> p (t e)")
                    t.matmul(misc[1][:, 0:TPQ * E], before[:], m, start=True, stop=True)
                    t.matmul(misc[1][:, TPQ * E:2 * TPQ * E], ones[:], m, start=True,
                             stop=True).then_inc(count_ps_ok, 1)

            def turn_x(i, par, half, first=False):
                pe.wait_ge(xs_in[par], 16 * half)
                if not first:
                    pe.wait_ge(hT_ok, 2 * (i - 1))
                for c in range(DC):
                    ins = t.transpose(xsT_ps[:, c * P:(c + 1) * P], xs[:, par, c * P:(c + 1) * P], ident[:])
                ins.then_inc(xsT_ps_ok, 1)

            def up(i, c2, e):
                pe.wait_ge(xsT_ok, i)
                for c in range(DC):
                    ins = t.matmul(h_ps[:, 512 * c2:512 * (c2 + 1)], xsT[:, c, :],
                                   w1_sb[:, bass.ds(e, 1), c, 512 * c2:512 * (c2 + 1)],
                                   start=(c == 0), stop=(c == DC - 1))
                ins.then_inc(h_ps_ok, 1)

            def down(i, e):
                pe.wait_ge(hT_ok, 2 * (i + 1))
                pe.wait_ge(y_ok, i + 1)
                for c in range(HC):
                    ins = t.matmul(y_ps, hgT[:, c, :], w2_sb[:, bass.ds(e, 1), c, :],
                                   start=(c == 0), stop=(c == HC - 1))
                ins.then_inc(y_ps_ok, 1)

            def turn_h(i, x_before=True):
                if x_before:
                    pe.wait_ge(xsT_ok, i + 1)
                for c2 in range(2):
                    pe.wait_ge(hg_ok, 2 * (i - 1) + c2 + 1)
                    for c in range(HC // 2 * c2, HC // 2 * (c2 + 1)):
                        ins = t.transpose(hT_ps[:, c * P:(c + 1) * P], hg[:, c * P:(c + 1) * P], ident[:])
                    ins.then_inc(hT_ps_ok, 1)

            def expert(i):
                return pe.value_load(tab_e[0:1, bass.ds(i, 1)], min_val=0, max_val=E - 1)

            def quarter(q, preparing, settling, tiles):
                if settling:
                    pe.wait_ge(rhoT_ok, q)
                for k in range(NBLK):
                    rho_block(q, k)
                    if preparing and k in PE_P:
                        prepare(PE_P[k][1], PE_P[k][0])
                    if settling and k in PE_S:
                        settle(PE_S[k], q - 1)
                    if tiles and k in PE_F:
                        m, step = PE_F[k]
                        i = tile(q, m)[0]
                        if step == "turn_x":
                            turn_x(*tile(q, m + 1))
                        elif step in ("up0", "up1"):
                            up(i, int(step[-1]), expert(i))
                        elif step == "down":
                            down(i - 1, expert(i - 1))
                        else:
                            turn_h(i)

            def step(this, following, mid=lambda: None):
                i = this[0]
                e = expert(i)
                up(i, 0, e)
                up(i, 1, e)
                mid()
                if following:
                    turn_x(*following)
                down(i - 1, expert(i - 1))
                turn_h(i, bool(following))

            pe.wait_ge(setup_sb, 4)
            prepare("turn", 0)
            prepare("project", 0)
            quarter(0, True, False, False)
            pe.wait_ge(feat_sb_ok, DC * NQ)
            quarter(1, False, True, False)
            pe.wait_ge(w_in, 16 * 2 * E)
            pe.wait_ge(table_ok, 1)
            turn_x(*tile_at(1), first=True)
            with pe.Fori(2, NQ) as q:
                quarter(q, False, True, True)
            settle("turn_scores", NQ - 1)
            mids = {TA + 1: "turn_x2", TA + 2: "logits", TA + 3: "count"}
            for i in range(TA, TB):
                step(tile_at(i), tile_at(i + 1),
                     lambda: settle(mids[i], NQ - 1) if i in mids else None)
            with pe.Fori(0, PAIRS) as n:
                step(tile_pair(n, 0), tile_pair(n, 1))
                step(tile_pair(n, 1), tile_pair(n, 2))
            step(tile_at(TE - 1), None)
            down(TE - 1, expert(TE - 1))

        @block.vector
        def _(dve):
            v = nc.vector
            loaded = (consts_in, 16 * N_CONST)
            v.memset(wpad[:], 0.0).then_inc(dve_const, 1)
            ctx4 = ctx_sb.rearrange("p c (b t) -> p (c b) t", b=B)
            v.memset(ctx4[:, :, T:TP], 0.0).then_inc(dve_const, 1)
            v.memset(mneg[:, :, T:TP], FILL).then_inc(dve_const, 1)
            dve.wait_ge(consts_in, 16 * N_CONST)
            dve.wait_ge(dve_const, 1)
            for c in range(DC):
                v.tensor_copy(wpad[:, c, 31:32], cols[:, 0, c:c + 1])
            v.tensor_scalar(mneg[:, :, 0:T], mask_i[:, :, 0:T], 1.0, NEG, ALU.subtract,
                            ALU.mult).then_inc(dve_const, 1)
            dve.wait_ge(pool_const, POOL_CONSTS)
            for k in range(2):
                for c in range(DC):
                    ins = v.tensor_scalar(wrep[:, k, c, :], ones[:], cols[:, 2 + k, c:c + 1], None, ALU.mult)
            ins.then_inc(dve_const, 1)
            v.tensor_copy(meta[:, 0, :], pad[:, D:ROW]).then_inc(meta_ok, 1)
            for g in range(2):
                v.tensor_scalar(region[:, g, :], iota8[:], float(CAP[g]), float(ROW0[g]), ALU.mult, ALU.add)
            v.memset(cum[:, 0, :], 0.0)
            dve.wait_ge(setup_ps, DC)
            for e in range(DC):
                v.tensor_scalar(txtb[:, e].rearrange("p b t -> p (b t)"), misc[0][:, e * B * TP:(e + 1) * B * TP],
                                cols[:, 1, e:e + 1], None, ALU.add).then_inc(setup_sb, 1)
            dve.wait_ge(setup_ps, DC + 2)
            for k in range(2):
                v.tensor_copy(cwb[:, :, k, :], misc[1][:, k * B * TP:(k + 1) * B * TP]
                              .rearrange("p (b t) -> p b t", b=B)).then_inc(setup_sb, 1)

            def prepare(step, q):
                link = Link(dve, p_link, P_LINKS * q)
                if step == "stats":
                    dve.wait_ge(x_in, 16 * (q + 1))
                    for n in range(TPQ):
                        ins = v.bn_stats(stats[:, n, :], xp[:, n, :])
                    link(ins)
                    for n in range(TPQ):
                        ins = v.bn_aggr(mv[:, TPQ * q + n, :], stats[:, n, :])
                    ins.then_inc(mv_ok, 1)
                    dve.wait_ge(mv_ok, q + 1)
                    v.tensor_scalar(var[:], mv[:, TPQ * q:TPQ * (q + 1), 1], EPS, None, ALU.add).then_inc(var1_ok, 1)
                elif step == "norm":
                    dve.wait_ge(rstd1_ok, q + 1)
                    for n in range(TPQ):
                        m = TPQ * q + n
                        ins = v.tensor_scalar(xn[:, n, :], xp[:, n, :], mv[:, m, 0:1], rstd[:, m:m + 1],
                                              ALU.subtract, ALU.mult)
                    ins.then_inc(xn_ok, 1)
                elif step == "turned":
                    for c in range(DC):
                        dve.wait_ge(xnT_ps_ok, DC * q + c + 1)
                        v.tensor_copy(xnT[:, c, :], misc[c][:]).then_inc(xnT_sb_ok, 1)
                else:
                    for e in range(DC):
                        dve.wait_ge(feat_ps_ok, DC * q + e + 1)
                        v.tensor_copy(featT[:, e, q, :], misc[e][:]).then_inc(feat_sb_ok, 1)

            def sum_block(q, k, bb):
                r, c = k // DC, k % DC
                if k >= HB:
                    dve.wait_ge(h_used, NBLK * q + k + 1 - HB)
                elif not (isinstance(q, int) and q == 0):
                    dve.wait_ge(h_used, NBLK * q + k + 1 - HB)
                for j in range(summed(k)[1]):
                    ins = v.tensor_scalar(hbuf[:, k % HB, j:j + 1, :], featT[:, c, bass.ds(q, 1), :],
                                          txtb[:, c, bb, CG * r + j:CG * r + j + 1], None, ALU.add)
                ins.then_inc(sum_ok, 1)

            def settle(step, q, bb, link, fresh=False):
                def wide(a, n, axis=2):
                    shape = list(a.shape)
                    shape.insert(axis, n)
                    return a.unsqueeze(axis).to_broadcast(shape)

                if step == "scores_out":
                    dve.wait_ge(h_used, NBLK * (q + 1))
                    v.tensor_copy(rhoT, rho[:]).then_inc(rhoT_ok, 1)
                elif step == "mask":
                    dve.wait_ge(rho_ps_ok, q + 1)
                    scores = misc[0][:].rearrange("p (n j r) -> p n r j", n=TPQ, j=CG)[:, :, 0:RS, :]
                    m = wide(mneg[:, bb if isinstance(bb, int) else bass.ds(bb, 1), :].rearrange(
                        "p (r j) -> p r j" if isinstance(bb, int) else "p o (r j) -> p (o r) j", j=CG), TPQ, 1)
                    link(v.tensor_tensor(sc[:].rearrange("p n (r j) -> p n r j", j=CG), scores, m, ALU.add))
                    link(v.tensor_reduce(mx[:], sc[:], AX.X, ALU.max))
                    v.tensor_tensor(sc[:], sc[:], wide(mx[:], TP), ALU.subtract).then_inc(shifted_ok, 1)
                elif step == "gates":
                    dve.wait_ge(exp_ok, q + 1)
                    v.tensor_reduce(den[:], sc[:], AX.X, ALU.add)
                    for k in range(2):
                        cw = cwb[:, bb, k, :] if isinstance(bb, int) else cwb[:, bass.ds(bb, 1), k, :].rearrange(
                            "p o t -> p (o t)")
                        ins = v.tensor_tensor(tmp[:, k], sc[:], wide(cw, TPQ, 1), ALU.mult)
                    link(ins)
                    v.reciprocal(den[:], den[:])
                    link(v.tensor_reduce(ws[:], tmp[:], AX.X, ALU.add))
                    link(v.tensor_tensor(ws[:], ws[:], wide(den[:], 2, 1), ALU.mult))
                    v.tensor_tensor(ws[:], ws[:], wide(gs[:, 2:4], TPQ), ALU.add).then_inc(ws_ok, 1)
                elif step == "x1":
                    dve.wait_ge(wt_ok, q + 1)
                    dve.wait_ge(gate_t, 1)
                    dve.wait_ge(xres_in, 16 * (q + 1))
                    link(v.tensor_scalar(wt[:], wt[:], tg[:, 0:1], None, ALU.mult))
                    link(v.tensor_tensor(ab[:, 0, :], wt[:, 0, :], rstd[:, bass.ds(TPQ * q, TPQ)], ALU.mult))
                    v.tensor_scalar(ab[:, 1, :], ab[:, 0, :], 1.0, None, ALU.add)
                    link(v.tensor_tensor(ab[:, 2, :], ab[:, 0, :], mv[:, bass.ds(TPQ * q, TPQ), 0], ALU.mult))
                    link(v.tensor_tensor(ab[:, 2, :], wt[:, 1, :], ab[:, 2, :], ALU.subtract))
                    for n in range(TPQ):
                        ins = v.tensor_scalar(x_res[:, n, :], x_res[:, n, :], ab[:, 1, n:n + 1], ab[:, 2, n:n + 1],
                                              ALU.mult, ALU.add)
                    link(ins, loaded)
                    for n in range(TPQ):
                        ins = v.bn_stats(stats2[:, n, :], x_res[:, n, :])
                    link(ins, loaded)
                    for n in range(TPQ):
                        ins = v.bn_aggr(mv2[:, n, :], stats2[:, n, :])
                    link(ins)
                    v.tensor_scalar(var2[:], mv2[:, :, 1], EPS, None, ALU.add).then_inc(x1_ok, 1)
                elif step == "x2":
                    dve.wait_ge(rstd2_ok, q + 1)
                    if not fresh:
                        dve.wait_ge(scattered, 16 * 2 * TPQ * q)
                    for n in range(TPQ):
                        ins = v.tensor_scalar(rows[:, n, 0:D], x_res[:, n, :], mv2[:, n, 0:1], rstd2[:, n:n + 1],
                                              ALU.subtract, ALU.mult)
                    ins.then_inc(x2_ok, 1)
                elif step == "x2T":
                    for c in range(DC):
                        dve.wait_ge(x2T_ps_ok, DC * q + c + 1)
                        v.tensor_copy(x2T[:, c, :], misc[c][:]).then_inc(x2T_sb_ok, 1)
                elif step == "top2":
                    dve.wait_ge(lg_ps_ok, q + 1)
                    link(v.tensor_copy(lg[:].rearrange("p t e -> p (t e)"), misc[0][:, 0:TPQ * E]), loaded)
                    for n in range(TPQ):
                        ins = v.max(top[:, n, :], lg[:, n, :])
                    link(ins, loaded)
                    for n in range(TPQ):
                        ins = v.max_index(topi[:, n, :], top[:, n, :], lg[:, n, :])
                    link(ins)
                    link(v.tensor_copy(topf[:], topi[:, :, 0:2]))
                    for k in range(2):
                        ins = v.tensor_tensor(pick[:, k], wide(iota8[:], TPQ, 1), wide(topf[:, :, k], E), ALU.is_equal)
                    link(ins)
                    v.tensor_tensor(dl[:], lg[:], wide(top[:, :, 0], E), ALU.subtract)
                    v.tensor_tensor(pick[:, 2], pick[:, 0], pick[:, 1], ALU.add).then_inc(pick_ok, 1)
                elif step == "place":
                    dve.wait_ge(rexp_ok, q + 1)
                    dve.wait_ge(pick_ok, q + 1)
                    link(v.tensor_reduce(zs[:], dl[:], AX.X, ALU.add))
                    v.reciprocal(zs[:], zs[:])
                    link(v.tensor_tensor(dl[:], dl[:], pick[:, 2], ALU.mult))
                    v.scalar_tensor_tensor(rows[:, :, D + 1:ROW], dl[:], tg[:, 1:2], wide(zs[:], E),
                                           ALU.mult, ALU.mult)
                    v.tensor_copy(rows[:, :, D].bitcast(I32), tokid[:, bass.ds(TPQ * q, TPQ)])
                    dve.wait_ge(count_ps_ok, q + 1)
                    g = 0 if isinstance(q, int) and q == 0 else 1
                    for n in range(TPQ):
                        link(v.tensor_tensor(cum[:, n + 1, :], cum[:, n, :],
                                             misc[1][:, (TPQ + n) * E:(TPQ + n + 1) * E], ALU.add))
                    link(v.tensor_tensor(pos[:], cum[:, 0:TPQ, :], misc[1][:, 0:TPQ * E]
                                         .rearrange("p (t e) -> p t e", e=E), ALU.add))
                    link(v.tensor_tensor(pos[:], pos[:], wide(region[:, g, :], TPQ, 1), ALU.add))
                    v.tensor_copy(cum[:, 0, :], cum[:, TPQ, :])
                    for k in range(2):
                        ins = v.tensor_tensor(sel[:, k], pos[:], pick[:, k], ALU.mult)
                    link(ins)
                    link(v.tensor_reduce(slotf[:], sel, AX.X, ALU.add))
                    v.tensor_copy(slot[:], slotf[:]).then_inc(rows_ok, 1)
                    dve.wait_ge(rows_ok, q + 1)
                    assert link.n == S_LINKS, link.n

            def table(g):
                link = Link(dve, r_link, R_LINKS * g)
                n = NTILES[g]
                first = (1, TB)[g]
                link(v.tensor_scalar(tl_i[:], cum[:, 0, :], 1.0 / P, (P - 1) / P - 0.498046875, ALU.mult, ALU.add))
                link(v.tensor_copy(tl[:, 0, :], tl_i[:]))
                link(v.tensor_tensor_scan(tl[:, 1, :], ones[:, 0:E], tl[:, 0, :], 0.0, ALU.mult, ALU.add))
                link(v.tensor_tensor(ind[:, 0, 0:n, :], tl[:, 1:2, :].to_broadcast([P, n, E]),
                                     iotan[:, 0:n].unsqueeze(2).to_broadcast([P, n, E]), ALU.is_le))
                link(v.tensor_tensor(ind[:, 1, 0:n, :], ind[:, 0, 0:n, :], tl[:, 0:1, :].to_broadcast([P, n, E]),
                                     ALU.mult))
                link(v.tensor_reduce(tabf[:, 0:2, 0:n], ind[:, :, 0:n, :], AX.X, ALU.add))
                v.tensor_scalar(tab_e[:, first:first + n], tabf[:, 0, 0:n], float(E - 1), None, ALU.min)
                link(v.tensor_tensor(tabf[:, 2, 0:n], iotan[:, 0:n], tabf[:, 1, 0:n], ALU.subtract))
                link(v.tensor_scalar(tabf[:, 2, 0:n], tabf[:, 2, 0:n], float(P), float(ROW0[g]), ALU.mult, ALU.add))
                v.scalar_tensor_tensor(tab_r[:, first:first + n], tabf[:, 0, 0:n], float(CAP[g]), tabf[:, 2, 0:n],
                                       ALU.mult, ALU.add)
                link(v.tensor_tensor(pad_r[:, g, :], region[:, g, :], cum[:, 0, :], ALU.add))
                v.memset(cum[:, 0, :], 0.0).then_inc(table_ok, 1)
                assert link.n == R_LINKS, link.n

            def turned_x(i):
                dve.wait_ge(xsT_ps_ok, i)
                v.tensor_copy(xsT[:].rearrange("p c k -> p (c k)"), xsT_ps).then_inc(xsT_ok, 1)

            def y_out(i, par):
                dve.wait_ge(y_ps_ok, i + 1)
                dve.wait_ge(added, 16 * (i + 1))
                dve.wait_ge(meta_ok, i + 1)
                e = dve.value_load(tab_e[0:1, bass.ds(i, 1)], min_val=0, max_val=E - 1)
                v.tensor_scalar(y_sb[:], y_ps, meta[:, par, bass.ds(e + 1, 1)], None, ALU.mult).then_inc(y_ok, 1)

            def keep_meta(i, par):
                dve.wait_ge(added, 16 * i)
                v.tensor_copy(meta[:, par, :], xs[:, par, D:ROW]).then_inc(meta_ok, 1)

            def turned_h(i):
                for c2 in range(2):
                    dve.wait_ge(hT_ps_ok, 2 * (i - 1) + c2 + 1)
                    v.tensor_copy(hgT[:].rearrange("p c k -> p (c k)")[:, 512 * c2:512 * (c2 + 1)],
                                  hT_ps[:, 512 * c2:512 * (c2 + 1)]).then_inc(hT_ok, 1)

            def quarter(q, bb, preparing, settling, tiles):
                dve.wait_ge(feat_sb_ok, DC * NQ if not preparing else DC)
                link = Link(dve, s_link, S_LINKS * (q - 1))
                for k in range(NBLK):
                    sum_block(q, k, bb)
                    if preparing and k in DVE_P:
                        prepare(DVE_P[k][1], DVE_P[k][0])
                    if settling and k in DVE_S:
                        fresh = isinstance(q, int) and q == 1
                        settle(DVE_S[k], q - 1, 0 if fresh else q - 2, link, fresh)
                        if fresh and DVE_S[k] == "place":
                            table(0)
                    if tiles and k in DVE_F:
                        m, step = DVE_F[k]
                        i, par, _ = tile(q, m)
                        if step == "x":
                            turned_x(i + 1)
                            keep_meta(i, par)
                        elif step == "y":
                            y_out(i - 1, 1 - par)
                        else:
                            turned_h(i)

            for s in ("stats", "norm", "turned", "projected"):
                prepare(s, 0)
            dve.wait_ge(setup_sb, 4)
            quarter(0, 0, True, False, False)
            quarter(1, 0, False, True, False)
            v.memset(hgT[:, 0:HC // 2, :], 0.0).then_inc(hT_ok, 1)
            v.memset(hgT[:, HC // 2:, :], 0.0).then_inc(hT_ok, 1)
            v.memset(y_sb[:], 0.0).then_inc(y_ok, 1)
            turned_x(1)
            with dve.Fori(2, NQ) as q:
                quarter(q, 1, False, True, True)
            link = Link(dve, s_link, S_LINKS * (NQ - 1))
            early = {TA: ("scores_out", "mask", "gates"), TA + 1: ("x1", "x2"), TA + 2: ("x2T",),
                     TA + 3: ("top2",), TA + 4: ("place",)}

            def step(i, par, following=True):
                if following:
                    turned_x(i + 1)
                keep_meta(i, par)
                turned_h(i)
                y_out(i - 1, 1 - par)

            for i in range(TA, TB):
                for s in early.get(i, ()):
                    settle(s, NQ - 1, 1, link)
                if i == TA + 4:
                    table(1)
                step(i, i % 2)
            with dve.Fori(0, PAIRS) as n:
                for u in range(2):
                    step(*tile_pair(n, u)[:2])
            step(TE - 1, (TE - 1) % 2, following=False)
            y_out(TE - 1, (TE - 1) % 2)


def kernel(**inputs):
    import numpy as np
    import concourse.bacc as bacc
    from concourse.bass_utils import run_bass_kernel_spmd

    a = {k: np.ascontiguousarray(v) for k, v in inputs.items()}

    def column(v):
        return v.reshape(DC, P).T

    laid = {
        "x": a["x"],
        "ctxT": a["ctx_1024"].transpose(2, 0, 1).reshape(DC, P, B, T).transpose(1, 0, 2, 3).reshape(P, DC * B, T),
        "mask": a["mask_BxS2_ik0"],
        "g_xattn": a["g_xattn"], "g_ffn": a["g_ffn"],
        "Ws": a["L0_xattn_Ws"], "W": a["L0_xattn_W"],
        "w": column(a["L0_xattn_w"]), "b": column(a["L0_xattn_b"]),
        "Wcw": column(a["L0_xattn_Wcw"]), "bcw": a["L0_xattn_bcw"],
        "Wcb": column(a["L0_xattn_Wcb"]), "bcb": a["L0_xattn_bcb"],
        "router": a["L0_ffn_router_w"].T.reshape(DC, P, E).transpose(1, 0, 2),
        "w1": a["L0_ffn_w1"].transpose(2, 0, 1).reshape(DC, P, E, H).transpose(1, 2, 0, 3),
        "w2": a["L0_ffn_w2"].transpose(2, 0, 1).reshape(HC, P, E, D).transpose(1, 2, 0, 3),
    }
    nc = bacc.Bacc("TRN2", target_bir_lowering=False, num_devices=1, dynamic_dma_scratch_size=8192)
    arrays, args = {}, []
    for name, v in laid.items():
        v = np.ascontiguousarray(v)
        arrays["in_" + name] = v
        args.append(nc.dram_tensor("in_" + name, v.shape, mybir.dt.from_np(v.dtype), kind="ExternalInput").ap())
    out = nc.dram_tensor("out_0", (NTOK + P, D), F32, kind="ExternalOutput").ap()
    flamingo_moe(nc, *args, out)
    r = run_bass_kernel_spmd(nc, [arrays], core_ids=[0])
    return r.results[0]["out_0"][:NTOK].reshape(B, S, D)
```

```python
from contextlib import ExitStack

import concourse.bass as bass
from concourse import mybir

ALU = mybir.AluOpType
ACT = mybir.ActivationFunctionType
AX = mybir.AxisListType
F32 = mybir.dt.float32
I32 = mybir.dt.int32
U32 = mybir.dt.uint32

P = 128
B, S, D, T = 2, 1024, 256, 77
E, H = 8, 1024
DC, HC = D // P, H // P
NTOK = B * S
QT = 512
NQ, TPQ = NTOK // QT, QT // P
CG = 4
RS = -(-T // CG)
TP = RS * CG
NBLK = RS * DC
HB = 4
NEG = 1e30
FILL = -3e38
EPS = 1e-5

def full_tiles(n):
    return -(-(2 * n * QT - E * (P - 1)) // P)


MAX_TILES = (2 * NTOK + E * (P - 1)) // P
FQ = 4
FC = 6
TA = 1 + 2 * FQ
TB = TA + FC
TABLE_TILES = (FQ - 1, FQ, FQ, TB - 3 * FQ)
SURE = 0
for _n, _q in zip(TABLE_TILES, (1, 2, 3, 3)):
    SURE = min(SURE + _n, full_tiles(_q))
NT_LAST = MAX_TILES - SURE
TE = TB + NT_LAST

CAP = NTOK + P
NFILL = TE - 1 - 2 * NTOK // P
NROWS = E * CAP + NFILL * P
META = 1 + E
ROW = D + META

S_LINKS = 27
P_LINKS = 1
R_LINKS = 11


def in_register(eng, value):
    return value if isinstance(value, int) else eng.to_reg(value)


class Link:

    def __init__(self, eng, sem, base):
        self.eng, self.sem, self.base, self.n = eng, sem, base, 0

    def __call__(self, ins, first=None):
        self.n += 1
        ins.then_inc(self.sem, 1)
        value = self.base + self.n
        if first:
            value = in_register(self.eng, value)
            self.eng.wait_ge(*first)
        self.eng.wait_ge(self.sem, value)


def flamingo_moe(nc, x, ctxT, mask, columns, scalars, Ws, W, router, w1, w2, out):
    with ExitStack() as ctx:
        def sb(name, shape, dt=F32):
            return ctx.enter_context(nc.sbuf_tensor(name, shape, dt))

        def sem(name):
            return ctx.enter_context(nc.semaphore(name))

        w1_sb = sb("w1_sb", [P, E, DC, H])
        w2_sb = sb("w2_sb", [P, E, HC, D])
        featT = sb("featT", [P, DC, NQ, QT])
        hbuf = sb("hbuf", [P, HB, CG, QT])
        x_res = sb("x_res", [P, TPQ, D])
        x2T = sb("x2T", [P, DC, QT])
        rows = sb("rows", [P, TPQ, ROW])
        W_sb = sb("W_sb", [P, DC, D])
        sc = sb("sc", [P, TPQ, TP])
        tmp = sb("tmp", [P, 2, TPQ, TP])
        rhoT = tmp[:].rearrange("p a t c -> p (a t c)")[:, 0:QT]
        ident = sb("ident", [P, P])
        before = sb("before", [P, P])
        ones = sb("ones", [P, P])
        wpad = sb("wpad", [P, DC, 64])
        txtb = sb("txtb", [P, DC, B, TP])
        cwb = sb("cwb", [P, B, 2, TP])
        mneg = sb("mneg", [P, B, TP])
        cols = sb("cols", [P, 4, DC])
        rT = sb("rT", [P, DC, E])
        gs = sb("gs", [P, 4])
        tg = sb("tg", [P, 2])
        negh = sb("negh", [P, TPQ])
        stats = sb("stats", [P, TPQ, 6])
        mv = sb("mv", [P, NTOK // P, 2])
        var = sb("var", [P, TPQ])
        rstd = sb("rstd", [P, NTOK // P])
        stats2 = sb("stats2", [P, TPQ, 6])
        mv2 = sb("mv2", [P, TPQ, 2])
        var2 = sb("var2", [P, TPQ])
        rstd2 = sb("rstd2", [P, TPQ])
        mx = sb("mx", [P, TPQ])
        den = sb("den", [P, TPQ])
        ws = sb("ws", [P, 2, TPQ])
        wt = sb("wt", [P, 2, TPQ])
        ab = sb("ab", [P, 3, TPQ])
        lg = sb("lg", [P, TPQ, E])
        top = sb("top", [P, TPQ, E])
        topi = sb("topi", [P, TPQ, E], U32)
        topf = sb("topf", [P, TPQ, 2])
        pick = sb("pick", [P, 3, TPQ, E])
        dl = sb("dl", [P, TPQ, E])
        zs = sb("zs", [P, TPQ])
        cum = sb("cum", [P, TPQ + 1, E])
        pos = sb("pos", [P, TPQ, E])
        sel = tmp[:].rearrange("p a t c -> p (a t c)")[:, 0:2 * TPQ * E].rearrange(
            "p (a t e) -> p a t e", a=2, t=TPQ)
        slotf = sb("slotf", [P, 2, TPQ])
        slot = sb("slot", [P, 2, TPQ], I32)
        region = sb("region", [P, E])
        tokid = sb("tokid", [P, NTOK // P], I32)
        iota8 = sb("iota8", [P, E])
        iotan = sb("iotan", [P, NT_LAST])
        tl_i = sb("tl_i", [P, E], I32)
        tl = sb("tl", [P, 4, E])
        worked = sb("worked", [P, E + 1])
        ind = tmp[:].rearrange("p a t c -> p (a t c)")[:, 0:2 * NT_LAST * E].rearrange(
            "p (a n e) -> p a n e", a=2, n=NT_LAST)
        tabf = sb("tabf", [P, 3, NT_LAST])
        tab_e = sb("tab_e", [P, TE], I32)
        tab_r = sb("tab_r", [P, TE], I32)
        pad_r = sb("pad_r", [P, E], I32)
        pad = sb("pad", [P, ROW])
        xs = sb("xs", [P, 2, ROW])
        xsT = sb("xsT", [P, DC, P])
        meta = sb("meta", [P, 2, META])
        hg = sb("hg", [P, H])
        hgT = sb("hgT", [P, HC, P])
        y_sb = sb("y_sb", [P, D])
        xp = hg[:].rearrange("p (t d) -> p t d", t=TPQ)
        xnT = hgT[:].rearrange("p c d -> p (c d)").rearrange("p (c k) -> p c k", c=DC)
        Ws_sb = x2T[:].rearrange("p c k -> p (c k)")[:, 0:DC * D].rearrange("p (c d) -> p c d", c=DC)
        ctx_sb = x2T[:].rearrange("p c k -> p (c k)")[:, DC * D:DC * (D + B * TP)].rearrange("p (c t) -> p c t", c=DC)
        wrep = x_res[:].rearrange("p t d -> p (t d)")[:, 0:2 * DC * P].rearrange("p (k c m) -> p k c m", k=2, c=DC)
        mask_i = sc[:, 0:B, :].bitcast(I32)
        xn = rows[:, :, 0:D]
        scratch = nc.dram_tensor("row_scratch", [NROWS, ROW], F32, kind="Internal").ap()

        def bank(name, n=1):
            return ctx.enter_context(nc.psum_tensor(name, [P, n * 512], F32))

        rho = bank("rho")
        misc = [bank("misc0"), bank("misc1")]
        h_ps = bank("h_ps", 2)
        hT_ps = bank("hT_ps", 2)
        y_bank = bank("y_bank")
        y_ps = y_bank[:, 0:D]
        xsT_ps = hT_ps[:, 0:D]

        consts_in = sem("consts_in")
        x_in = sem("x_in")
        text_in = sem("text_in")
        W_in = sem("W_in")
        w_in = sem("w_in")
        fill_in = sem("fill_in")
        pads_in = sem("pads_in")
        pool_const = sem("pool_const")
        dve_const = sem("dve_const")
        gate_t = sem("gate_t")
        setup_ps = sem("setup_ps")
        setup_sb = sem("setup_sb")
        p_link = sem("p_link")
        mv_ok = sem("mv_ok")
        s_link = sem("s_link")
        r_link = sem("r_link")
        var1_ok = sem("var1_ok")
        rstd1_ok = sem("rstd1_ok")
        xn_ok = sem("xn_ok")
        xnT_ps_ok = sem("xnT_ps_ok")
        xnT_sb_ok = sem("xnT_sb_ok")
        feat_ps_ok = sem("feat_ps_ok")
        feat_sb_ok = sem("feat_sb_ok")
        sum_ok = sem("sum_ok")
        h_ok = sem("h_ok")
        h_used = sem("h_used")
        rhoT_ok = sem("rhoT_ok")
        rho_ps_ok = sem("rho_ps_ok")
        shifted_ok = sem("shifted_ok")
        exp_ok = sem("exp_ok")
        ws_ok = sem("ws_ok")
        wt_ok = sem("wt_ok")
        xres_in = sem("xres_in")
        x1_ok = sem("x1_ok")
        x1_out = sem("x1_out")
        rstd2_ok = sem("rstd2_ok")
        x2_ok = sem("x2_ok")
        x2T_ps_ok = sem("x2T_ps_ok")
        x2T_sb_ok = sem("x2T_sb_ok")
        lg_ps_ok = sem("lg_ps_ok")
        pick_ok = sem("pick_ok")
        rexp_ok = sem("rexp_ok")
        count_ps_ok = sem("count_ps_ok")
        rows_ok = sem("rows_ok")
        scattered = sem("scattered")
        table_ok = sem("table_ok")
        xs_in = [sem("xs_in0"), sem("xs_in1")]
        xsT_ps_ok = sem("xsT_ps_ok")
        xsT_ok = sem("xsT_ok")
        h_ps_ok = sem("h_ps_ok")
        hg_ok = sem("hg_ok")
        hT_ps_ok = sem("hT_ps_ok")
        hT_ok = sem("hT_ok")
        meta_ok = sem("meta_ok")
        y_ps_ok = sem("y_ps_ok")
        y_ok = sem("y_ok")
        added = sem("added")

        N_CONST = 4
        POOL_CONSTS = 11
        DVE_CONSTS = 5
        x_rows = x.rearrange("b s d -> (b s) d").rearrange("(t p) d -> p t d", p=P)
        out_rows = out.rearrange("(t p) d -> p t d", p=P)

        PE_P = {13 * k + d: (k + 1, s) for k in range(NQ - 1)
                for d, s in ((1, "turn"), (4, "project0"), (6, "project1"))}
        DVE_P = {13 * k + d: (k + 1, s) for k in range(NQ - 1)
                 for d, s in ((0, "stats"), (3, "norm"), (6, "turned"), (9, "projected0"), (11, "projected1"))}
        PE_S = {0: "turn_scores", 13: "turn_x2", 15: "logits", 18: "count"}
        ACT_S = {6: "exp", 8: "tanh", 19: "exp_router"}
        DVE_S = {5: "mask", 8: "gates", 10: "x1", 12: "stats", 14: "x2", 17: "x2T", 20: "top2",
                 22: "place", 24: "table"}
        def steps(**at):
            table = {k: (m, name) for name, ks in at.items() for m, k in enumerate(ks)}
            assert len(table) == FQ * len(at)
            return table

        PE_F = steps(up0=(4, 11, 19, 29), up1=(5, 12, 20, 30), down0=(7, 14, 22, 32), down1=(8, 15, 23, 33),
                     turn_h=(9, 17, 25, 35))
        PE_X = {6: 0, 13: 1, 27: 2, 31: 3}
        LATE = 2
        ACT_F = steps(gelu0=(6, 13, 21, 31), gelu1=(7, 14, 22, 32))
        DVE_F = steps(x=(10, 17, 30, 35), meta=(9, 16, 27, 36), y=(12, 19, 28, 37), h=(14, 21, 29, 39))
        DIRECT = (range(0, NBLK, 3), range(30), range(27))

        def summed(q, k):
            n = CG if k // DC < RS - 1 else T - CG * (RS - 1)
            return n, n - (1 if n == CG and k in DIRECT[q if isinstance(q, int) else -1] else 0)

        def tile(q, m):
            return FQ * (q - 2) + 1 + m, (1 + m) % 2, FQ // 2 * (q - 2) + (m + 2) // 2

        def tile_at(i):
            return i, i % 2, (i + 1) // 2

        def tile_pair(n, u):
            return TB + 2 * n + u, (TB + u) % 2, n + (TB + u + 1) // 2

        PAIRS = (TE - 1 - TB) // 2
        assert (TE - 1 - TB) % 2 == 0 and FQ % 2 == 0

        block = ctx.enter_context(nc.Block())

        @block.sync
        def _(sp):
            sp.dma_start(xp, x_rows[:, 0:TPQ, :]).then_inc(x_in, 16)
            sp.dma_start(Ws_sb, Ws.rearrange("(c p) e -> p c e", p=P)).then_inc(text_in, 16)
            sp.dma_start(ctx_sb.rearrange("p c (b t) -> p (c b) t", b=B)[:, :, 0:T], ctxT).then_inc(text_in, 16)
            sp.dma_start(cols[:], columns).then_inc(consts_in, 16)
            sp.dma_start(W_sb[:], W.rearrange("(c p) e -> p c e", p=P)).then_inc(W_in, 16)
            sp.dma_start(mask_i[:, :, 0:T], mask.partition_broadcast(P)).then_inc(consts_in, 16)
            sp.dma_start(gs[:], scalars.partition_broadcast(P)).then_inc(consts_in, 16)
            sp.dma_start(rT[:], router).then_inc(consts_in, 16)
            for q in range(1, NQ):
                sp.wait_ge(xn_ok, q)
                sp.dma_start(xp, x_rows[:, TPQ * q:TPQ * (q + 1), :]).then_inc(x_in, 16)
            for e in range(E):
                sp.dma_start(w1_sb[:, e], w1[:, e]).then_inc(w_in, 16)
                sp.dma_start(w2_sb[:, e], w2[:, e]).then_inc(w_in, 16)
            sp.wait_ge(pool_const, POOL_CONSTS)
            for n in range(NFILL):
                r0 = E * CAP + n * P
                sp.dma_start(scratch[r0:r0 + P, :], pad[:]).then_inc(fill_in, 16)

            def res_load(q, first=False):
                if first:
                    sp.wait_ge(setup_ps, 4)
                else:
                    sp.wait_ge(x1_out, 16 * q)
                    sp.wait_ge(x2_ok, q)
                sp.dma_start(x_res[:], x_rows[:, bass.ds(TPQ * q, TPQ), :]).then_inc(xres_in, 16)

            def x1_store(q):
                sp.wait_ge(x1_ok, q + 1)
                sp.dma_start(out_rows[:, bass.ds(TPQ * q, TPQ), :], x_res[:]).then_inc(x1_out, 16)

            def settled(q, tables):
                tables, rows_there, x1_there = (in_register(sp, n) for n in (
                    tables, 16 * 2 * TPQ * (q + 1), 16 * (q + 1)))
                sp.wait_ge(table_ok, tables)
                sp.wait_ge(scattered, rows_there)
                sp.wait_ge(x1_out, x1_there)

            def xs_load(i, par, half):
                if not (isinstance(i, int) and i == 1):
                    sp.wait_ge(meta_ok, i - 1)
                r = sp.value_load(tab_r[0:1, bass.ds(i, 1)], min_val=0, max_val=NROWS - P)
                sp.dma_start(xs[:, par, :], scratch[bass.ds(r, P), :]).then_inc(xs_in[par], 16)

            res_load(0, first=True)
            x1_store(0)
            sp.wait_ge(fill_in, 16 * NFILL)
            settled(0, 1)
            xs_load(*tile_at(1))
            with sp.Fori(2, NQ) as q:
                res_load(q - 1)
                xs_load(*tile(q, 1))
                x1_store(q - 1)
                xs_load(*tile(q, 2))
                settled(q - 1, q)
                xs_load(*tile(q, 3))
                xs_load(*tile(q, 4))
            res_load(NQ - 1)
            xs_load(*tile_at(TA + 1))
            xs_load(*tile_at(TA + 2))
            x1_store(NQ - 1)
            sp.wait_ge(table_ok, NQ)
            for i in range(TA + 3, TB):
                xs_load(*tile_at(i))
            sp.wait_ge(table_ok, NQ + 1)
            for e in range(E):
                r = sp.value_load(pad_r[0:1, e:e + 1], min_val=0, max_val=NROWS - P)
                sp.dma_start(scratch[bass.ds(r, P), :], pad[:]).then_inc(pads_in, 16)
            sp.wait_ge(pads_in, 16 * E)
            settled(NQ - 1, NQ + 1)
            xs_load(*tile_at(TB))
            xs_load(*tile_at(TB + 1))
            with sp.Fori(0, PAIRS - 1) as n:
                xs_load(*tile_pair(n + 1, 0))
                xs_load(*tile_pair(n + 1, 1))
            xs_load(*tile_at(TE - 1))
            sp.wait_ge(x1_out, 16 * NQ)

        @block.gpsimd
        def _(pool):
            g = nc.gpsimd
            g.memset(negh[:], -0.5).then_inc(pool_const, 1)
            g.memset(ident[:], 0.0).then_inc(pool_const, 1)
            g.memset(ones[:], 1.0).then_inc(pool_const, 1)
            pool.wait_ge(pool_const, 3)
            g.affine_select(out=ident[:], in_=ident[:], compare_op=ALU.not_equal, fill=1.0, base=0,
                            pattern=[[-1, P]], channel_multiplier=1).then_inc(pool_const, 1)
            g.affine_select(out=before[:], in_=ones[:], compare_op=ALU.is_gt, fill=0.0, base=0,
                            pattern=[[1, P]], channel_multiplier=-1).then_inc(pool_const, 1)
            g.iota(tokid[:], pattern=[[P, NTOK // P]], base=0, channel_multiplier=1).then_inc(pool_const, 1)
            g.iota(iota8[:], pattern=[[1, E]], base=0, channel_multiplier=0,
                   allow_small_or_imprecise_dtypes=True).then_inc(pool_const, 1)
            g.iota(iotan[:], pattern=[[1, NT_LAST]], base=0, channel_multiplier=0,
                   allow_small_or_imprecise_dtypes=True).then_inc(pool_const, 1)
            g.memset(pad[:], 0.0).then_inc(pool_const, 1)
            g.memset(tab_e[:, 0:1], 0).then_inc(pool_const, 1)
            pool.wait_ge(pool_const, 9)
            g.iota(pad[:, D:D + 1].bitcast(I32), pattern=[[0, 1]], base=NTOK,
                   channel_multiplier=1).then_inc(pool_const, 1)

            pool.wait_ge(pool_const, POOL_CONSTS)
            pool.dma_start(out[NTOK:NTOK + P, :], pad[:, 0:D]).then_inc(added, 16)

            for q in range(NQ):
                pool.wait_ge(var1_ok, q + 1)
                g.tensor_tensor(rstd[:, TPQ * q:TPQ * (q + 1)], var[:], negh[:], ALU.pow).then_inc(rstd1_ok, 1)

            def root(q):
                pool.wait_ge(x1_ok, q + 1)
                g.tensor_tensor(rstd2[:], var2[:], negh[:], ALU.pow).then_inc(rstd2_ok, 1)

            def scatter(q):
                count = in_register(pool, q + 1)
                pool.wait_ge(pool_const, POOL_CONSTS)
                pool.wait_ge(rows_ok, count)
                for t in range(TPQ):
                    for k in range(2):
                        g.indirect_dma_start(
                            out=scratch, out_offset=bass.IndirectOffsetOnAxis(ap=slot[:, k, t:t + 1], axis=0),
                            in_=rows[:, t, :], in_offset=None).then_inc(scattered, 16)

            def add(i, par, half):
                y_count, add_count = in_register(pool, i + 2), in_register(pool, 16 * (i + 1))
                pool.wait_ge(pool_const, POOL_CONSTS)
                pool.wait_ge(y_ok, y_count)
                pool.wait_ge(added, add_count)
                g.indirect_dma_start(
                    out=out, out_offset=bass.IndirectOffsetOnAxis(ap=meta[:, par, 0:1].bitcast(I32), axis=0),
                    in_=y_sb[:], in_offset=None, compute_op=ALU.add).then_inc(added, 16)

            root(0)
            scatter(0)
            with pool.Fori(2, NQ) as q:
                add(*tile(q, -1))
                root(q - 1)
                add(*tile(q, 0))
                scatter(q - 1)
                add(*tile(q, 1))
                add(*tile(q, 2))
            for i in range(TA, TB):
                add(*tile_at(i - 1))
                if i == TA:
                    root(NQ - 1)
                if i == TA + 2:
                    scatter(NQ - 1)
            with pool.Fori(0, PAIRS) as n:
                add(*tile_pair(n, -1))
                add(*tile_pair(n, 0))
            add(*tile_at(TE - 2))
            add(*tile_at(TE - 1))
            pool.wait_ge(added, 16 * (TE + 1))

        @block.scalar
        def _(act):
            s = nc.scalar
            act.wait_ge(consts_in, 16 * N_CONST)
            s.activation(tg[:], gs[:, 0:2], ACT.Tanh).then_inc(gate_t, 1)

            def tanh_block(q, k, bb):
                act.wait_ge(sum_ok, NBLK * q + k + 1)
                n, m = summed(q, k)
                r, c = k // DC, k % DC
                h = hbuf[:, k % HB, 0:m, :]
                ins = s.activation(h, h, ACT.Tanh)
                for j in range(m, n):
                    ins = s.activation(hbuf[:, k % HB, j, :], featT[:, c, bass.ds(q, 1), :].rearrange("p o t -> p (o t)"),
                                       ACT.Tanh, bias=txtb[:, c, bb, CG * r + j:CG * r + j + 1])
                ins.then_inc(h_ok, 1)

            def settle(step, q):
                if step == "exp":
                    act.wait_ge(shifted_ok, q + 1)
                    s.activation(sc[:], sc[:], ACT.Exp).then_inc(exp_ok, 1)
                elif step == "tanh":
                    act.wait_ge(ws_ok, q + 1)
                    s.activation(wt[:], ws[:], ACT.Tanh).then_inc(wt_ok, 1)
                elif step == "exp_router":
                    act.wait_ge(pick_ok, q + 1)
                    s.activation(dl[:], dl[:], ACT.Exp).then_inc(rexp_ok, 1)

            def gelu(i, c):
                act.wait_ge(h_ps_ok, 2 * (i - 1) + c + 1)
                s.activation(hg[:, 512 * c:512 * (c + 1)], h_ps[:, 512 * c:512 * (c + 1)],
                             ACT.Gelu).then_inc(hg_ok, 1)

            def quarter(q, bb, settling, tiles):
                for k in range(NBLK):
                    tanh_block(q, k, bb)
                    if settling and k in ACT_S:
                        settle(ACT_S[k], q - 1)
                    if tiles and k in ACT_F:
                        m, step = ACT_F[k]
                        gelu(tile(q, m)[0], int(step[-1]))

            quarter(0, 0, False, False)
            quarter(1, 0, True, False)
            with act.Fori(2, NQ) as q:
                quarter(q, 1, True, True)
            for i in range(TA, TB):
                if i == TA:
                    settle("exp", NQ - 1)
                gelu(i, 0)
                gelu(i, 1)
                if i == TA:
                    settle("tanh", NQ - 1)
                if i == TA + 2:
                    settle("exp_router", NQ - 1)
            with act.Fori(0, PAIRS) as n:
                for u in range(2):
                    gelu(tile_pair(n, u)[0], 0)
                    gelu(tile_pair(n, u)[0], 1)
            gelu(TE - 1, 0)
            gelu(TE - 1, 1)

        @block.tensor
        def _(pe):
            t = nc.tensor

            pe.wait_ge(text_in, 16 * 2)
            pe.wait_ge(dve_const, 2)
            for e in range(DC):
                for c in range(DC):
                    ins = t.matmul(misc[0][:, e * B * TP:(e + 1) * B * TP], Ws_sb[:, c, e * P:(e + 1) * P],
                                   ctx_sb[:, c, :], start=(c == 0), stop=(c == DC - 1))
                ins.then_inc(setup_ps, 1)

            def gate_projections():
                pe.wait_ge(dve_const, DVE_CONSTS)
                for k in range(2):
                    for c in range(DC):
                        ins = t.matmul(h_ps[:, k * B * TP:(k + 1) * B * TP], wrep[:, k, c, :],
                                       ctx_sb[:, c, :], start=(c == 0), stop=(c == DC - 1))
                    ins.then_inc(setup_ps, 1)

            def prepare(step, q):
                if step == "turn":
                    pe.wait_ge(xn_ok, q + 1)
                    for c in range(DC):
                        if q:
                            pe.wait_ge(feat_sb_ok, DC * (q - 1) + c + 1)
                        for n in range(TPQ):
                            ins = t.transpose(misc[c][:, n * P:(n + 1) * P], xn[:, n, c * P:(c + 1) * P], ident[:])
                        ins.then_inc(xnT_ps_ok, 1)
                else:
                    if q == 0:
                        pe.wait_ge(W_in, 16)
                    e = int(step[-1])
                    pe.wait_ge(xnT_sb_ok, DC * (q + 1))
                    for c in range(DC):
                        ins = t.matmul(misc[e][:], W_sb[:, c, e * P:(e + 1) * P], xnT[:, c, :],
                                       start=(c == 0), stop=(c == DC - 1))
                    ins.then_inc(feat_ps_ok, 1)

            def rho_block(q, k):
                r, c = k // DC, k % DC
                pe.wait_ge(h_ok, NBLK * q + k + 1)
                n = CG if r < RS - 1 else T - CG * (RS - 1)
                for j in range(n):
                    last = r == RS - 1 or (r == RS - 2 and j >= T - CG * (RS - 1))
                    ins = t.matmul(rho[32 * j:32 * j + 32, :], wpad[:, c, 31 - r:63 - r], hbuf[:, k % HB, j, :],
                                   start=(k == 0), stop=(last and c == DC - 1), skip_group_check=True)
                ins.then_inc(h_used, 1)

            def settle(step, q):
                if step == "turn_scores":
                    pe.wait_ge(rhoT_ok, q + 1)
                    for n in range(TPQ):
                        ins = t.transpose(misc[0][:, n * P:(n + 1) * P], rhoT[:, n * P:(n + 1) * P], ident[:])
                    ins.then_inc(rho_ps_ok, 1)
                elif step == "turn_x2":
                    pe.wait_ge(x2_ok, q + 1)
                    for c in range(DC):
                        for n in range(TPQ):
                            ins = t.transpose(misc[c][:, n * P:(n + 1) * P], rows[:, n, c * P:(c + 1) * P], ident[:])
                        ins.then_inc(x2T_ps_ok, 1)
                elif step == "logits":
                    pe.wait_ge(x2T_sb_ok, DC * (q + 1))
                    for n in range(TPQ):
                        for c in range(DC):
                            ins = t.matmul(misc[0][:, n * E:(n + 1) * E], x2T[:, c, n * P:(n + 1) * P],
                                           rT[:, c, :], start=(c == 0), stop=(c == DC - 1))
                    ins.then_inc(lg_ps_ok, 1)
                elif step == "count":
                    pe.wait_ge(pick_ok, q + 1)
                    m = pick[:, 2].rearrange("p t e -> p (t e)")
                    t.matmul(misc[1][:, 0:TPQ * E], before[:], m, start=True, stop=True)
                    t.matmul(misc[1][:, TPQ * E:2 * TPQ * E], ones[:], m, start=True,
                             stop=True).then_inc(count_ps_ok, 1)

            def turn_x(i, par, half, late=False):
                pe.wait_ge(xs_in[par], 16 * half)
                if late:
                    pe.wait_ge(hT_ok, 2 * i)
                elif not (isinstance(i, int) and i == 1):
                    pe.wait_ge(hT_ok, 2 * (i - 1))
                for c in range(DC):
                    ins = t.transpose(xsT_ps[:, c * P:(c + 1) * P], xs[:, par, c * P:(c + 1) * P], ident[:])
                ins.then_inc(xsT_ps_ok, 1)

            def up(i, c2, e):
                pe.wait_ge(xsT_ok, i)
                for c in range(DC):
                    ins = t.matmul(h_ps[:, 512 * c2:512 * (c2 + 1)], xsT[:, c, :],
                                   w1_sb[:, bass.ds(e, 1), c, 512 * c2:512 * (c2 + 1)],
                                   start=(c == 0), stop=(c == DC - 1))
                ins.then_inc(h_ps_ok, 1)

            def down(i, half, e):
                if half == 0:
                    pe.wait_ge(hT_ok, 2 * (i + 1))
                    pe.wait_ge(y_ok, i + 1)
                for c in range(HC // 2 * half, HC // 2 * (half + 1)):
                    ins = t.matmul(y_ps, hgT[:, c, :], w2_sb[:, bass.ds(e, 1), c, :],
                                   start=(c == 0), stop=(c == HC - 1))
                if half == 1:
                    ins.then_inc(y_ps_ok, 1)

            def turn_h(i, x_before=True):
                if x_before:
                    pe.wait_ge(xsT_ok, i + 1)
                for c2 in range(2):
                    pe.wait_ge(hg_ok, 2 * (i - 1) + c2 + 1)
                    for c in range(HC // 2 * c2, HC // 2 * (c2 + 1)):
                        ins = t.transpose(hT_ps[:, c * P:(c + 1) * P], hg[:, c * P:(c + 1) * P], ident[:])
                    ins.then_inc(hT_ps_ok, 1)

            def expert(i):
                return pe.value_load(tab_e[0:1, bass.ds(i, 1)], min_val=0, max_val=E - 1)

            def quarter(q, preparing, settling, tiles):
                if settling:
                    pe.wait_ge(rhoT_ok, q)
                for k in range(NBLK):
                    rho_block(q, k)
                    if preparing and k in PE_P:
                        prepare(PE_P[k][1], PE_P[k][0])
                    if settling and k in PE_S:
                        settle(PE_S[k], q - 1)
                    if k in PE_X and (tiles or settling and k == max(PE_X)):
                        turn_x(*tile(q, PE_X[k] + 1), late=(PE_X[k] == LATE))
                    if tiles and k in PE_F:
                        m, step = PE_F[k]
                        i = tile(q, m)[0]
                        if step in ("up0", "up1"):
                            up(i, int(step[-1]), expert(i))
                        elif step in ("down0", "down1"):
                            down(i - 1, int(step[-1]), expert(i - 1))
                        else:
                            turn_h(i, x_before=(m != LATE))

            def step(this, following, mid=lambda: None, late=lambda: None):
                i = this[0]
                e = expert(i)
                up(i, 0, e)
                up(i, 1, e)
                mid()
                if following:
                    turn_x(*following)
                e = expert(i - 1)
                down(i - 1, 0, e)
                down(i - 1, 1, e)
                late()
                turn_h(i, bool(following))

            pe.wait_ge(setup_sb, DC)
            prepare("turn", 0)
            prepare("project0", 0)
            prepare("project1", 0)
            gate_projections()
            quarter(0, True, False, False)
            pe.wait_ge(feat_sb_ok, DC * NQ)
            quarter(1, False, True, False)
            pe.wait_ge(w_in, 16 * 2 * E)
            with pe.Fori(2, NQ) as q:
                quarter(q, False, True, True)
            settle("turn_scores", NQ - 1)
            for i in range(TA, TB):
                if i == TA + 2:
                    settle("turn_x2", NQ - 1)
                    step(tile_at(i), tile_at(i + 1), mid=lambda: settle("logits", NQ - 1),
                         late=lambda: settle("count", NQ - 1))
                else:
                    step(tile_at(i), tile_at(i + 1))
            with pe.Fori(0, PAIRS) as n:
                step(tile_pair(n, 0), tile_pair(n, 1))
                step(tile_pair(n, 1), tile_pair(n, 2))
            step(tile_at(TE - 1), None)
            e = expert(TE - 1)
            down(TE - 1, 0, e)
            down(TE - 1, 1, e)

        @block.vector
        def _(dve):
            v = nc.vector
            loaded = (consts_in, 16 * N_CONST)
            v.memset(wpad[:], 0.0).then_inc(dve_const, 1)
            ctx4 = ctx_sb.rearrange("p c (b t) -> p (c b) t", b=B)
            v.memset(ctx4[:, :, T:TP], 0.0).then_inc(dve_const, 1)
            v.memset(mneg[:, :, T:TP], FILL).then_inc(dve_const, 1)

            def constants():
                dve.wait_ge(consts_in, 16 * N_CONST)
                dve.wait_ge(dve_const, 1)
                for c in range(DC):
                    v.tensor_copy(wpad[:, c, 31:32], cols[:, 0, c:c + 1])
                v.tensor_scalar(mneg[:, :, 0:T], mask_i[:, :, 0:T], 1.0, NEG, ALU.subtract,
                                ALU.mult).then_inc(dve_const, 1)
                dve.wait_ge(pool_const, POOL_CONSTS)
                for k in range(2):
                    for c in range(DC):
                        ins = v.tensor_scalar(wrep[:, k, c, :], ones[:], cols[:, 2 + k, c:c + 1], None, ALU.mult)
                ins.then_inc(dve_const, 1)
                v.tensor_copy(meta[:, 0, :], pad[:, D:ROW]).then_inc(meta_ok, 1)
                v.tensor_scalar(region[:], iota8[:], float(CAP), None, ALU.mult)
                v.memset(cum[:, 0, :], 0.0)
                v.memset(worked[:], 0.0)
                dve.wait_ge(setup_ps, DC)
                for e in range(DC):
                    v.tensor_scalar(txtb[:, e].rearrange("p b t -> p (b t)"),
                                    misc[0][:, e * B * TP:(e + 1) * B * TP], cols[:, 1, e:e + 1], None,
                                    ALU.add).then_inc(setup_sb, 1)

            def gate_projections():
                dve.wait_ge(setup_ps, DC + 2)
                for k in range(2):
                    v.tensor_copy(cwb[:, :, k, :], h_ps[:, k * B * TP:(k + 1) * B * TP]
                                  .rearrange("p (b t) -> p b t", b=B)).then_inc(setup_sb, 1)

            def prepare(step, q):
                link = Link(dve, p_link, P_LINKS * q)
                if step == "stats":
                    dve.wait_ge(x_in, 16 * (q + 1))
                    for n in range(TPQ):
                        ins = v.bn_stats(stats[:, n, :], xp[:, n, :])
                    link(ins)
                    for n in range(TPQ):
                        ins = v.bn_aggr(mv[:, TPQ * q + n, :], stats[:, n, :])
                    ins.then_inc(mv_ok, 1)
                    dve.wait_ge(mv_ok, q + 1)
                    v.tensor_scalar(var[:], mv[:, TPQ * q:TPQ * (q + 1), 1], EPS, None, ALU.add).then_inc(var1_ok, 1)
                elif step == "norm":
                    dve.wait_ge(rstd1_ok, q + 1)
                    for n in range(TPQ):
                        m = TPQ * q + n
                        ins = v.tensor_scalar(xn[:, n, :], xp[:, n, :], mv[:, m, 0:1], rstd[:, m:m + 1],
                                              ALU.subtract, ALU.mult)
                    ins.then_inc(xn_ok, 1)
                elif step == "turned":
                    for c in range(DC):
                        dve.wait_ge(xnT_ps_ok, DC * q + c + 1)
                        v.tensor_copy(xnT[:, c, :], misc[c][:]).then_inc(xnT_sb_ok, 1)
                else:
                    e = int(step[-1])
                    dve.wait_ge(feat_ps_ok, DC * q + e + 1)
                    v.tensor_copy(featT[:, e, q, :], misc[e][:]).then_inc(feat_sb_ok, 1)

            def sum_block(q, k, bb):
                r, c = k // DC, k % DC
                if k >= HB:
                    dve.wait_ge(h_used, NBLK * q + k + 1 - HB)
                elif not (isinstance(q, int) and q == 0):
                    dve.wait_ge(h_used, NBLK * q + k + 1 - HB)
                for j in range(summed(q, k)[1]):
                    ins = v.tensor_scalar(hbuf[:, k % HB, j:j + 1, :], featT[:, c, bass.ds(q, 1), :],
                                          txtb[:, c, bb, CG * r + j:CG * r + j + 1], None, ALU.add)
                ins.then_inc(sum_ok, 1)

            def settle(step, q, bb, link, fresh=False):
                def wide(a, n, axis=2):
                    shape = list(a.shape)
                    shape.insert(axis, n)
                    return a.unsqueeze(axis).to_broadcast(shape)

                if step == "scores_out":
                    dve.wait_ge(h_used, NBLK * (q + 1))
                    v.tensor_copy(rhoT, rho[:]).then_inc(rhoT_ok, 1)
                elif step == "mask":
                    dve.wait_ge(rho_ps_ok, q + 1)
                    scores = misc[0][:].rearrange("p (n j r) -> p n r j", n=TPQ, j=CG)[:, :, 0:RS, :]
                    m = wide(mneg[:, bb if isinstance(bb, int) else bass.ds(bb, 1), :].rearrange(
                        "p (r j) -> p r j" if isinstance(bb, int) else "p o (r j) -> p (o r) j", j=CG), TPQ, 1)
                    link(v.tensor_tensor(sc[:].rearrange("p n (r j) -> p n r j", j=CG), scores, m, ALU.add))
                    link(v.tensor_reduce(mx[:], sc[:], AX.X, ALU.max))
                    v.tensor_tensor(sc[:], sc[:], wide(mx[:], TP), ALU.subtract).then_inc(shifted_ok, 1)
                elif step == "gates":
                    dve.wait_ge(exp_ok, q + 1)
                    v.tensor_reduce(den[:], sc[:], AX.X, ALU.add)
                    for k in range(2):
                        cw = cwb[:, bb, k, :] if isinstance(bb, int) else cwb[:, bass.ds(bb, 1), k, :].rearrange(
                            "p o t -> p (o t)")
                        ins = v.tensor_tensor(tmp[:, k], sc[:], wide(cw, TPQ, 1), ALU.mult)
                    link(ins)
                    v.reciprocal(den[:], den[:])
                    link(v.tensor_reduce(ws[:], tmp[:], AX.X, ALU.add))
                    link(v.tensor_tensor(ws[:], ws[:], wide(den[:], 2, 1), ALU.mult))
                    v.tensor_tensor(ws[:], ws[:], wide(gs[:, 2:4], TPQ), ALU.add).then_inc(ws_ok, 1)
                elif step == "x1":
                    dve.wait_ge(wt_ok, q + 1)
                    dve.wait_ge(gate_t, 1)
                    dve.wait_ge(xres_in, 16 * (q + 1))
                    link(v.tensor_scalar(wt[:], wt[:], tg[:, 0:1], None, ALU.mult))
                    link(v.tensor_tensor(ab[:, 0, :], wt[:, 0, :], rstd[:, bass.ds(TPQ * q, TPQ)], ALU.mult))
                    v.tensor_scalar(ab[:, 1, :], ab[:, 0, :], 1.0, None, ALU.add)
                    link(v.tensor_tensor(ab[:, 2, :], ab[:, 0, :], mv[:, bass.ds(TPQ * q, TPQ), 0], ALU.mult))
                    link(v.tensor_tensor(ab[:, 2, :], wt[:, 1, :], ab[:, 2, :], ALU.subtract))
                    for n in range(TPQ):
                        ins = v.tensor_scalar(x_res[:, n, :], x_res[:, n, :], ab[:, 1, n:n + 1], ab[:, 2, n:n + 1],
                                              ALU.mult, ALU.add)
                    link(ins, loaded)
                elif step == "stats":
                    for n in range(TPQ):
                        ins = v.bn_stats(stats2[:, n, :], x_res[:, n, :])
                    link(ins, loaded)
                    for n in range(TPQ):
                        ins = v.bn_aggr(mv2[:, n, :], stats2[:, n, :])
                    link(ins)
                    v.tensor_scalar(var2[:], mv2[:, :, 1], EPS, None, ALU.add).then_inc(x1_ok, 1)
                elif step == "x2":
                    dve.wait_ge(rstd2_ok, q + 1)
                    if not fresh:
                        dve.wait_ge(scattered, 16 * 2 * TPQ * q)
                    for n in range(TPQ):
                        ins = v.tensor_scalar(rows[:, n, 0:D], x_res[:, n, :], mv2[:, n, 0:1], rstd2[:, n:n + 1],
                                              ALU.subtract, ALU.mult)
                    ins.then_inc(x2_ok, 1)
                elif step == "x2T":
                    for c in range(DC):
                        dve.wait_ge(x2T_ps_ok, DC * q + c + 1)
                        v.tensor_copy(x2T[:, c, :], misc[c][:]).then_inc(x2T_sb_ok, 1)
                elif step == "top2":
                    dve.wait_ge(lg_ps_ok, q + 1)
                    link(v.tensor_copy(lg[:].rearrange("p t e -> p (t e)"), misc[0][:, 0:TPQ * E]), loaded)
                    for n in range(TPQ):
                        ins = v.max(top[:, n, :], lg[:, n, :])
                    link(ins, loaded)
                    for n in range(TPQ):
                        ins = v.max_index(topi[:, n, :], top[:, n, :], lg[:, n, :])
                    link(ins)
                    link(v.tensor_copy(topf[:], topi[:, :, 0:2]))
                    for k in range(2):
                        ins = v.tensor_tensor(pick[:, k], wide(iota8[:], TPQ, 1), wide(topf[:, :, k], E), ALU.is_equal)
                    link(ins)
                    v.tensor_tensor(dl[:], lg[:], wide(top[:, :, 0], E), ALU.subtract)
                    v.tensor_tensor(pick[:, 2], pick[:, 0], pick[:, 1], ALU.add).then_inc(pick_ok, 1)
                elif step == "place":
                    dve.wait_ge(rexp_ok, q + 1)
                    dve.wait_ge(pick_ok, q + 1)
                    link(v.tensor_reduce(zs[:], dl[:], AX.X, ALU.add))
                    v.reciprocal(zs[:], zs[:])
                    link(v.tensor_tensor(dl[:], dl[:], pick[:, 2], ALU.mult))
                    v.scalar_tensor_tensor(rows[:, :, D + 1:ROW], dl[:], tg[:, 1:2], wide(zs[:], E),
                                           ALU.mult, ALU.mult)
                    v.tensor_copy(rows[:, :, D].bitcast(I32), tokid[:, bass.ds(TPQ * q, TPQ)])
                    dve.wait_ge(count_ps_ok, q + 1)
                    for n in range(TPQ):
                        link(v.tensor_tensor(cum[:, n + 1, :], cum[:, n, :],
                                             misc[1][:, (TPQ + n) * E:(TPQ + n + 1) * E], ALU.add))
                    link(v.tensor_tensor(pos[:], cum[:, 0:TPQ, :], misc[1][:, 0:TPQ * E]
                                         .rearrange("p (t e) -> p t e", e=E), ALU.add))
                    link(v.tensor_tensor(pos[:], pos[:], wide(region[:], TPQ, 1), ALU.add))
                    v.tensor_copy(cum[:, 0, :], cum[:, TPQ, :])
                    for k in range(2):
                        ins = v.tensor_tensor(sel[:, k], pos[:], pick[:, k], ALU.mult)
                    link(ins)
                    link(v.tensor_reduce(slotf[:], sel, AX.X, ALU.add))
                    v.tensor_copy(slot[:], slotf[:]).then_inc(rows_ok, 1)
                    dve.wait_ge(rows_ok, q + 1)
                    assert link.n == S_LINKS, link.n

            def table(nth, first, n, full=True):
                link = Link(dve, r_link, R_LINKS * nth)
                shift = -0.498046875 + (0 if full else (P - 1) / P)
                link(v.tensor_scalar(tl_i[:], cum[:, 0, :], 1.0 / P, shift, ALU.mult, ALU.add))
                link(v.tensor_copy(tl[:, 2, :], tl_i[:]))
                v.tensor_tensor(tl[:, 3, :], tl[:, 2, :], worked[:, 1:E + 1], ALU.subtract)
                link(v.tensor_tensor(tl[:, 0, :], tl[:, 2, :], worked[:, 0:E], ALU.subtract))
                link(v.tensor_tensor_scan(tl[:, 1, :], ones[:, 0:E], tl[:, 0, :], 0.0, ALU.mult, ALU.add))
                v.tensor_tensor(tl[:, 2, :], tl[:, 1, :], tl[:, 0, :], ALU.subtract)
                link(v.tensor_tensor(ind[:, 0, 0:n, :], tl[:, 1:2, :].to_broadcast([P, n, E]),
                                     iotan[:, 0:n].unsqueeze(2).to_broadcast([P, n, E]), ALU.is_le))
                v.tensor_scalar(tl[:, 2, :], tl[:, 2, :], -1.0, float(n), ALU.mult, ALU.add)
                link(v.tensor_tensor(ind[:, 1, 0:n, :], ind[:, 0, 0:n, :], tl[:, 3:4, :].to_broadcast([P, n, E]),
                                     ALU.mult))
                v.scalar_tensor_tensor(tl[:, 2, :], tl[:, 2, :], 0.0, tl[:, 0, :], ALU.max, ALU.min)
                link(v.tensor_reduce(tabf[:, 0:2, 0:n], ind[:, :, 0:n, :], AX.X, ALU.add))
                v.tensor_scalar(tab_e[:, bass.ds(first, n)], tabf[:, 0, 0:n], float(E - 1), None, ALU.min)
                link(v.scalar_tensor_tensor(tabf[:, 2, 0:n], iotan[:, 0:n], worked[:, 0:1], tabf[:, 1, 0:n],
                                            ALU.add, ALU.subtract))
                link(v.tensor_scalar(tabf[:, 2, 0:n], tabf[:, 2, 0:n], float(P), None, ALU.mult))
                link(v.scalar_tensor_tensor(tab_r[:, bass.ds(first, n)], tabf[:, 0, 0:n], float(CAP), tabf[:, 2, 0:n],
                                            ALU.mult, ALU.add))
                if not full:
                    link(v.tensor_tensor(pad_r[:], region[:], cum[:, 0, :], ALU.add))
                else:
                    link(v.tensor_tensor(worked[:, 0:E], worked[:, 0:E], tl[:, 2, :], ALU.add))
                v.memset(tabf[:, 0, 0:1], 0.0).then_inc(table_ok, 1)
                assert link.n == R_LINKS, link.n

            def turned_x(i):
                dve.wait_ge(xsT_ps_ok, i)
                v.tensor_copy(xsT[:].rearrange("p c k -> p (c k)"), xsT_ps).then_inc(xsT_ok, 1)

            def y_out(i, par):
                dve.wait_ge(y_ps_ok, i + 1)
                dve.wait_ge(added, 16 * (i + 1))
                dve.wait_ge(meta_ok, i + 1)
                e = dve.value_load(tab_e[0:1, bass.ds(i, 1)], min_val=0, max_val=E - 1)
                v.tensor_scalar(y_sb[:], y_ps, meta[:, par, bass.ds(e + 1, 1)], None, ALU.mult).then_inc(y_ok, 1)

            def keep_meta(i, par):
                dve.wait_ge(added, 16 * i)
                v.tensor_copy(meta[:, par, :], xs[:, par, D:ROW]).then_inc(meta_ok, 1)

            def turned_h(i):
                for c2 in range(2):
                    dve.wait_ge(hT_ps_ok, 2 * (i - 1) + c2 + 1)
                    v.tensor_copy(hgT[:].rearrange("p c k -> p (c k)")[:, 512 * c2:512 * (c2 + 1)],
                                  hT_ps[:, 512 * c2:512 * (c2 + 1)]).then_inc(hT_ok, 1)

            EMPTY = 30

            def quarter(q, bb, preparing, settling, tiles):
                dve.wait_ge(feat_sb_ok, DC * NQ if not preparing else 1)
                link = Link(dve, s_link, S_LINKS * (q - 1))
                for k in range(NBLK):
                    if k == 3 and settling:
                        settle("scores_out", q - 1, 0, link)
                    sum_block(q, k, bb)
                    if preparing and k == 0:
                        prepare("projected1", 0)
                        dve.wait_ge(feat_sb_ok, DC)
                    if preparing and k == 4:
                        gate_projections()
                    if preparing and k in DVE_P:
                        prepare(DVE_P[k][1], DVE_P[k][0])
                    if settling and k in DVE_S:
                        fresh = isinstance(q, int) and q == 1
                        if DVE_S[k] != "table":
                            settle(DVE_S[k], q - 1, 0 if fresh else q - 2, link, fresh)
                        else:
                            table(q - 1, 1 + (FQ - 1 if not fresh else 0) + (FQ * (q - 2) if not fresh else 0),
                                  TABLE_TILES[0] if fresh else FQ)
                    if settling and not tiles and k == EMPTY:
                        v.memset(hgT[:, 0:HC // 2, :], 0.0).then_inc(hT_ok, 1)
                        v.memset(hgT[:, HC // 2:, :], 0.0).then_inc(hT_ok, 1)
                        v.memset(y_sb[:], 0.0).then_inc(y_ok, 1)
                    if settling and not tiles and k in DVE_F and DVE_F[k] == (FQ - 1, "x"):
                        turned_x(1)
                    if tiles and k in DVE_F:
                        m, step = DVE_F[k]
                        i, par, _ = tile(q, m)
                        if step == "x":
                            turned_x(i + 1)
                        elif step == "meta":
                            keep_meta(i, par)
                        elif step == "y":
                            y_out(i - 1, 1 - par)
                        else:
                            turned_h(i)

            prepare("stats", 0)
            constants()
            prepare("norm", 0)
            prepare("turned", 0)
            prepare("projected0", 0)
            dve.wait_ge(setup_sb, DC)
            quarter(0, 0, True, False, False)
            quarter(1, 0, False, True, False)
            with dve.Fori(2, NQ) as q:
                quarter(q, 1, False, True, True)
            link = Link(dve, s_link, S_LINKS * (NQ - 1))

            def step(i, par, following=True, before=(), middle=(), behind=()):
                for s in before:
                    settle(s, NQ - 1, 1, link)
                if following:
                    turned_x(i + 1)
                keep_meta(i, par)
                for s in middle:
                    settle(s, NQ - 1, 1, link)
                if isinstance(i, int) and i == TA + 1:
                    table(NQ - 1, 3 * FQ, TABLE_TILES[3])
                turned_h(i)
                y_out(i - 1, 1 - par)
                for s in behind:
                    settle(s, NQ - 1, 1, link)

            step(TA, TA % 2, before=("scores_out", "mask"), middle=("gates",), behind=("x1", "stats"))
            step(TA + 1, (TA + 1) % 2, middle=("x2",), behind=("x2T",))
            step(TA + 2, TA % 2, middle=("top2",), behind=("place",))
            table(NQ, TB, NT_LAST, full=False)
            for i in range(TA + 3, TB):
                step(i, i % 2)
            with dve.Fori(0, PAIRS) as n:
                for u in range(2):
                    step(*tile_pair(n, u)[:2])
            step(TE - 1, (TE - 1) % 2, following=False)
            y_out(TE - 1, (TE - 1) % 2)


def kernel(**inputs):
    import numpy as np
    import concourse.bacc as bacc
    from concourse.bass_utils import run_bass_kernel_spmd

    a = {k: np.ascontiguousarray(v) for k, v in inputs.items()}

    def column(v):
        return v.reshape(DC, P).T

    laid = {
        "x": a["x"],
        "ctxT": a["ctx_1024"].transpose(2, 0, 1).reshape(DC, P, B, T).transpose(1, 0, 2, 3).reshape(P, DC * B, T),
        "mask": a["mask_BxS2_ik0"],
        "columns": np.stack([column(a["L0_xattn_" + n]) for n in ("w", "b", "Wcw", "Wcb")], axis=1),
        "scalars": np.concatenate([a["g_xattn"], a["g_ffn"], a["L0_xattn_bcw"], a["L0_xattn_bcb"]]),
        "Ws": a["L0_xattn_Ws"], "W": a["L0_xattn_W"],
        "router": a["L0_ffn_router_w"].T.reshape(DC, P, E).transpose(1, 0, 2),
        "w1": a["L0_ffn_w1"].transpose(2, 0, 1).reshape(DC, P, E, H).transpose(1, 2, 0, 3),
        "w2": a["L0_ffn_w2"].transpose(2, 0, 1).reshape(HC, P, E, D).transpose(1, 2, 0, 3),
    }
    nc = bacc.Bacc("TRN2", target_bir_lowering=False, num_devices=1, dynamic_dma_scratch_size=8192)
    arrays, args = {}, []
    for name, v in laid.items():
        v = np.ascontiguousarray(v)
        arrays["in_" + name] = v
        args.append(nc.dram_tensor("in_" + name, v.shape, mybir.dt.from_np(v.dtype), kind="ExternalInput").ap())
    out = nc.dram_tensor("out_0", (NTOK + P, D), F32, kind="ExternalOutput").ap()
    flamingo_moe(nc, *args, out)
    r = run_bass_kernel_spmd(nc, [arrays], core_ids=[0])
    return r.results[0]["out_0"][:NTOK].reshape(B, S, D)
```
